# Optimizing a Trainium2 kernel written in Bass

```python
import numpy as np
import jax
import jax.numpy as jnp

def _softmax(x, axis=-1):
    return jax.nn.softmax(x, axis=axis)

def _gelu(x):
    return jax.nn.gelu(x, approximate=True)

def _silu(x):
    return jax.nn.silu(x)

def _sigmoid(x):
    return jax.nn.sigmoid(x)

def _layernorm(x, axis=-1, eps=1e-05):
    m = jnp.mean(x, axis=axis, keepdims=True)
    v = jnp.var(x, axis=axis, keepdims=True)
    return (x - m) / jnp.sqrt(v + eps)

def _scatter_add(tgt, idx, src, axis=0):
    return tgt.at[idx].add(src)

def _segment_sum(src, seg, n):
    return jax.ops.segment_sum(src, seg, n)
kernel_name = 'mk_adj_preln_d1_adj_r2_5d5061'

def setup_inputs(seed: int=0):
    np.random.seed(seed)
    _w = jnp.asarray

    def _rec_inputs():
        import jax
        import jax.numpy as jnp
        _gk = jax.random.key(seed)
        x = -0.0005207 + 1.001 * jax.random.normal(jax.random.fold_in(_gk, 1), (8, 1024, 128), jnp.float32)
        _a = jax.random.bernoulli(jax.random.fold_in(_gk, 2), 0.00195312, (8, 1024, 1024))
        _a = jnp.logical_or(_a, jnp.swapaxes(_a, -1, -2))
        _a = jnp.logical_or(_a, jnp.eye(1024, dtype=bool))
        adj = _a.astype(jnp.int32)
        return (x, adj)
    x, adj = _rec_inputs()

    def _L0_gnn_setup():
        import jax, jax.numpy as jnp
        import numpy as np
        B, N, IN_F, OUT_F, H, NUM_EDGE_TYPES = (16, 256, 128, 128, 8, 50)
        HEAD_DIM = OUT_F // H
        LN_EPS = 1e-05
        key = jax.random.key(seed)
        ks = jax.random.split(key, 8)
        x = jax.random.normal(ks[0], (B, N, IN_F), dtype=jnp.float32)
        adj = jax.random.randint(ks[1], (B, N, N), 0, 2, dtype=jnp.int32)
        edge_types = jax.random.randint(ks[2], (B, N, N), 0, NUM_EDGE_TYPES, dtype=jnp.int32)
        W = jax.random.normal(ks[3], (IN_F, OUT_F), dtype=jnp.float32) / np.sqrt(IN_F)
        a1 = jax.random.normal(ks[4], (HEAD_DIM,), dtype=jnp.float32) / np.sqrt(HEAD_DIM)
        a2 = jax.random.normal(ks[5], (HEAD_DIM,), dtype=jnp.float32) / np.sqrt(HEAD_DIM)
        edge_emb = jax.random.normal(ks[6], (NUM_EDGE_TYPES, H), dtype=jnp.float32) * 0.02
        edge_emb = edge_emb.at[0].set(0.0)
        ln_gamma = jnp.ones((OUT_F,), dtype=jnp.float32)
        ln_beta = jnp.zeros((OUT_F,), dtype=jnp.float32)
        return {'x': x, 'adj': adj, 'edge_types': edge_types, 'W': W, 'a1': a1, 'a2': a2, 'edge_emb': edge_emb, 'ln_gamma': ln_gamma, 'ln_beta': ln_beta}
    _L0_gnn_all = _L0_gnn_setup()
    _L0_gnn_in = {k: v for k, v in _L0_gnn_all.items() if k in ('W', 'a1', 'a2', 'edge_emb', 'ln_gamma', 'ln_beta')}
    del _L0_gnn_all
    return {'x': x, 'adj': adj, 'L0_gnn_W': _L0_gnn_in['W'], 'L0_gnn_a1': _L0_gnn_in['a1'], 'L0_gnn_a2': _L0_gnn_in['a2'], 'L0_gnn_edge_emb': _L0_gnn_in['edge_emb'], 'L0_gnn_ln_gamma': _L0_gnn_in['ln_gamma'], 'L0_gnn_ln_beta': _L0_gnn_in['ln_beta']}

def reference(x, adj, L0_gnn_W, L0_gnn_a1, L0_gnn_a2, L0_gnn_edge_emb, L0_gnn_ln_gamma, L0_gnn_ln_beta):
    import jax
    import jax.numpy as jnp

    def _L0_gnn_ref(x, adj, edge_types, W, a1, a2, edge_emb, ln_gamma, ln_beta):
        import jax, jax.numpy as jnp
        import numpy as np
        B, N, IN_F, OUT_F, H, NUM_EDGE_TYPES = (16, 256, 128, 128, 8, 50)
        HEAD_DIM = OUT_F // H
        LN_EPS = 1e-05
        Bx, Nx, _ = x.shape
        Wh = (x @ W).reshape(Bx, Nx, H, HEAD_DIM)
        s1 = jnp.einsum('bnhd,d->bnh', Wh, a1)
        s2 = jnp.einsum('bnhd,d->bnh', Wh, a2)
        e = s1[:, :, None, :] + s2[:, None, :, :] + edge_emb[edge_types]
        e = jnp.where(e > 0, e, 0.2 * e)
        e = jnp.where((adj == 0)[..., None], jnp.float32(-1000000000.0), e)
        alpha = jax.nn.softmax(e, axis=2)
        h = jnp.einsum('bijh,bjhd->bihd', alpha, Wh).reshape(Bx, Nx, OUT_F)
        mu = jnp.mean(h, axis=-1, keepdims=True)
        var = jnp.mean(jnp.square(h - mu), axis=-1, keepdims=True)
        hn = (h - mu) * jax.lax.rsqrt(var + LN_EPS) * ln_gamma + ln_beta
        return jax.nn.elu(hn)
    h = jnp.maximum(_layernorm(x, axis=-1), 0.0)
    x = x + _L0_gnn_ref(h, adj, adj, L0_gnn_W, L0_gnn_a1, L0_gnn_a2, L0_gnn_edge_emb, L0_gnn_ln_gamma, L0_gnn_ln_beta)
    return x

_drawn_inputs = setup_inputs


def setup_inputs(seed=0):
    import zlib

    import numpy as np

    out = dict(_drawn_inputs(seed))
    spreads = {'L0_gnn_ln_gamma': (1.0, 0.2), 'L0_gnn_ln_beta': (0.0, 0.1)}
    factors = {'L0_gnn_edge_emb': 32.15}
    for name, (base, spread) in spreads.items():
        noise = np.random.default_rng([zlib.crc32(name.encode()), seed]).standard_normal(out[name].shape)
        drawn = base * np.exp(spread * noise) if base else spread * noise
        out[name] = jnp.asarray(drawn.astype(out[name].dtype))
    for name, factor in factors.items():
        out[name] = (out[name] * factor).astype(out[name].dtype)
    return out
```

```python
import numpy as np
import concourse.bass as bass
from concourse import mybir
from contextlib import ExitStack

F32 = mybir.dt.float32
BF16 = mybir.dt.bfloat16
FP8 = mybir.dt.float8e4
U32 = mybir.dt.uint32
U8 = mybir.dt.uint8
ALU = mybir.AluOpType
ACT = mybir.ActivationFunctionType
AX = mybir.AxisListType


def gat_block(nc, x, adj, W, a1, a2, edge_emb, gamma, beta, out):
    Bn, N, F = x.shape
    H = edge_emb.shape[1]
    DH = F // H
    P = 128
    T = N // P
    R = 4
    K = T // R
    V = DH + 1
    C = 2 * V
    PARTS = 3
    CP = PARTS * C
    PITCH = 128
    BANK = 512
    NG = 4
    SLOPE = 0.2
    EPS = 1e-5
    BIG = float(2 ** 60)
    RHO_CAP = 100.0
    DVE_UNITS = [2, 1, 1, 1, 1, 1, 1, 2]
    DVE_G = sum(DVE_UNITS)
    ACT_G = H * T - DVE_G

    s1_rows = nc.dram_tensor("s1_rows", (2, H, N), F32, kind="Internal").ap()

    ctx = ExitStack()
    with ctx:
        def sb(name, shape, dt):
            return ctx.enter_context(nc.sbuf_tensor(name, shape, dt))

        def pb(name, shape, dt):
            return ctx.enter_context(nc.psum_tensor(name, shape, dt))

        def sem(name):
            return ctx.enter_context(nc.semaphore(name))

        ident = sb("ident", [P, P], F32)
        ones = sb("ones", [16, P], F32)
        w_sb = sb("w_sb", [P, F], F32)
        a12 = sb("a12", [P, 2, DH], F32)
        wa_prod = sb("wa_prod", [P, 2, F], F32)
        w_s = sb("w_s", [P, 2 * H], F32)
        edge = sb("edge", [P, H], F32)
        gam = sb("gam", [P, F], F32)
        bet = sb("bet", [P, F], F32)
        x_ln = sb("x_ln", [P, T, F], F32)
        x_res = sb("x_res", [P, T, F], F32)
        stats = sb("stats", [P, T, 6], F32)
        mv = sb("mv", [P, T, 2], F32)
        rs = sb("rs", [P, T], F32)
        rs_t = sb("rs_t", [P, T], F32)
        xn = sb("xn", [P, T, F], F32)
        hT = sb("hT", [P, N], F32)
        hsum = sb("hsum", [P, 1], F32)
        hsum_rep = sb("hsum_rep", [P, P], F32)
        s1n = sb("s1n", [P, T, H], F32)
        s2n = sb("s2n", [P, T, H], F32)
        thr = [sb(f"thr{p}", [P, T, H], F32) for p in range(2)]
        bigs2 = [sb(f"bigs2{p}", [P, T, H], F32) for p in range(2)]
        wsum = [sb(f"wsum{p}", [P, H, V], F32) for p in range(2)]
        sT = sb("sT", [H, N], F32)
        smax = sb("smax", [2 * H, 1], F32)
        smax_diag = sb("smax_diag", [2 * H, H], F32)
        m_bc = sb("m_bc", [P, H], F32)
        expo = sb("expo", [P, 3, T, H], F32)
        bd = sb("bd", [P, 2, T, H], F32)
        rho = [sb(f"rho{p}", [P, T, H], F32) for p in range(2)]
        s1bc = sb("s1bc", [P, H, N], F32)
        xf = sb("xf", [P, T * H, C], F32)
        xp = [sb(f"xp{p}", [P, T, H, PARTS, C], BF16) for p in range(2)]
        adj8 = sb("adj8", [P, T, N], U8)
        mask = [sb(f"mask{p}", [P, K, N], U32) for p in range(2)]
        g = sb("g", [P, NG, K, N], U32)
        sumg = [sb(f"sumg{p}", [P, T, H, C], F32) for p in range(2)]
        summ = [sb(f"summ{p}", [P, T, H * V], F32) for p in range(2)]
        lone = sb("lone", [P, T], F32)
        num = sb("num", [P, T * H, V], F32)
        rden = sb("rden", [P, T * H], F32)
        agg = sb("agg", [P, T, F], F32)
        stats2 = sb("stats2", [P, T, 6], F32)
        mv2 = sb("mv2", [P, T, 2], F32)
        rs2 = sb("rs2", [P, T], F32)
        rs2_t = sb("rs2_t", [P, T], F32)
        e_out = sb("e_out", [P, T, F], F32)
        y = sb("y", [P, T, F], F32)

        acc = [pb(f"acc{q}", [P, T, PITCH], F32) for q in range(2)]
        mps = pb("mps", [P, 2, BANK], F32)
        fps = pb("fps", [P, 2 * BANK], F32)

        g8 = g[:, :, :, :].bitcast(FP8).rearrange("p n k (i r) -> p n k i r", r=R)
        mask8 = [m[:, :, :].bitcast(FP8).rearrange("p k (i r) -> p k i r", r=R) for m in mask]
        adj_w = adj8[:, :, :].bitcast(F32)

        const_ld = sem("const_ld")
        x_ln_ld = sem("x_ln_ld")
        x_res_ld = sem("x_res_ld")
        adj_ld = sem("adj_ld")
        s1_st = sem("s1_st")
        s1bc_ld = [sem(f"s1bc_ld{q}") for q in range(H // 2)]
        out_st = sem("out_st")
        ident_zero = sem("ident_zero")
        consts = sem("consts")
        waits_met = sem("waits_met")
        ws_prod = sem("ws_prod")
        ws_done = sem("ws_done")
        ln_stats = sem("ln_stats")
        ln_mv = sem("ln_mv")
        ln_ln = sem("ln_ln")
        ln_rs0 = sem("ln_rs0")
        ln_newton = sem("ln_newton")
        ln_done = sem("ln_done")
        hT_ps = sem("hT_ps")
        hT_done = sem("hT_done")
        hrep_done = sem("hrep_done")
        s_ps = sem("s_ps")
        sT_ps = sem("sT_ps")
        s_kept = sem("s_kept")
        thr_done = sem("thr_done")
        wsum_done = sem("wsum_done")
        sT_done = sem("sT_done")
        smax_done = sem("smax_done")
        diag_done = sem("diag_done")
        m_ps = sem("m_ps")
        m_done = sem("m_done")
        expo_step = sem("expo_step")
        exp_done = sem("exp_done")
        wh_ps = sem("wh_ps")
        xf_done = sem("xf_done")
        hi_done = sem("hi_done")
        rest1 = sem("rest1")
        mid_done = sem("mid_done")
        xp_done = sem("xp_done")
        mask_ps = sem("mask_ps")
        mask_done = sem("mask_done")
        gen_act = sem("gen_act")
        gen_dve = sem("gen_dve")
        g_done = sem("g_done")
        acc_done = sem("acc_done")
        sumg_done = sem("sumg_done")
        mterm_ps = sem("mterm_ps")
        summ_done = sem("summ_done")
        p_sub = sem("p_sub")
        p_lone = sem("p_lone")
        p_rho = sem("p_rho")
        p_add = sem("p_add")
        p_fix = sem("p_fix")
        p_rden = sem("p_rden")
        p_agg = sem("p_agg")
        p_stats = sem("p_stats")
        p_mv = sem("p_mv")
        p_ln = sem("p_ln")
        p_rs0 = sem("p_rs0")
        p_newton = sem("p_newton")
        p_norm = sem("p_norm")
        p_gam = sem("p_gam")
        p_z = sem("p_z")
        p_exp = sem("p_exp")
        p_y = sem("p_y")
        p_out = sem("p_out")

        def nodes(ap2d):
            return ap2d.rearrange("(k p r) f -> p k r f", k=K, p=P)

        def tiles(t):
            return t.rearrange("p (k r) f -> p k r f", k=K)

        def graph(ap, b):
            return ap[b, :, :] if isinstance(b, int) else ap[bass.ds(b, 1), :, :].rearrange("a n f -> (a n) f")

        block = ctx.enter_context(nc.Block())

        def settle(eng):
            eng.sem_inc(waits_met, 1)

        def each_batch(eng, batch):
            batch(0, 0, True, False)
            with eng.Fori(0, Bn // 2 - 1) as i:
                batch(i * 2 + 1, 1, True, True)
                batch(i * 2 + 2, 0, True, True)
            batch(Bn - 1, 1, False, True)

        @block.sync
        def _(sp):
            sp.dma_start(x_ln[:, :, :].rearrange("p (k r) f -> p k r f", k=K), nodes(x[0, :, :])).then_inc(x_ln_ld, 16)
            sp.dma_start(w_sb[:, :], W).then_inc(const_ld, 16)
            for c, v in enumerate((a1, a2)):
                sp.dma_start(a12[:, c, :], v.rearrange("(a d) -> a d", a=1).broadcast_to([P, DH])).then_inc(const_ld, 16)
            sp.dma_start(edge[:, :], edge_emb[1:2, :].broadcast_to([P, H])).then_inc(const_ld, 16)
            for t_, v in ((gam, gamma), (bet, beta)):
                sp.dma_start(t_[:, :], v.rearrange("(a d) -> a d", a=1).broadcast_to([P, F])).then_inc(const_ld, 16)

            def scores_out(n, p):
                sp.wait_ge(sT_done, n + 1)
                sp.dma_start(s1_rows[p, :, :], sT[:, :]).then_inc(s1_st, 16)
                sp.wait_ge(s1_st, (n + 1) * 16)
                for q in range(H // 2):
                    if not (isinstance(n, int) and n == 0):
                        sp.wait_ge(gen_act, (n - 1) * ACT_G + ACT_G - sum(T - u for u in DVE_UNITS[2 * q + 2:]))
                        settle(sp)
                        sp.wait_ge(gen_dve, (n - 1) * DVE_G + sum(DVE_UNITS[:2 * q + 2]))
                        settle(sp)
                    sp.dma_start(s1bc[:, 2 * q:2 * q + 2, :],
                                 s1_rows[p:p + 1, 2 * q:2 * q + 2, :].broadcast_to([P, 2, N])).then_inc(s1bc_ld[q], 16)

            def load_x_ln(n):
                sp.wait_ge(ln_done, n)
                sp.dma_start(tiles(x_ln[:, :, :]), nodes(graph(x, n))).then_inc(x_ln_ld, 16)

            def store_out(n):
                sp.wait_ge(p_out, n + 1)
                sp.dma_start(nodes(graph(out, n)), tiles(y[:, :, :])).then_inc(out_st, 16)

            def load_x_res(n):
                if not (isinstance(n, int) and n == 0):
                    sp.wait_ge(p_y, n)
                sp.dma_start(tiles(x_res[:, :, :]), nodes(graph(x, n))).then_inc(x_res_ld, 16)

            scores_out(0, 0)

            def batch(b, p, front, post):
                if front:
                    load_x_ln(b + 1)
                if post:
                    store_out(b - 1)
                load_x_res(b)
                if front:
                    scores_out(b + 1, 1 - p)

            each_batch(sp, batch)
            store_out(Bn - 1)
            sp.wait_ge(out_st, Bn * 16)

        @block.gpsimd
        def _(pool):
            pool.memset(ident[:, :], 0.0).then_inc(ident_zero, 1)
            pool.memset(ones[:, :], 1.0).then_inc(consts, 1)
            pool.wait_ge(ident_zero, 1)
            pool.affine_select(out=ident[:, :], in_=ident[:, :], compare_op=ALU.not_equal, fill=1.0, base=0,
                               pattern=[[-1, P]], channel_multiplier=1).then_inc(consts, 1)
            for w in wsum:
                pool.memset(w[:, :, DH:V], float(N)).then_inc(consts, 1)

            def load_adj(n):
                pool.dma_start(tiles(adj8[:, :, :]), nodes(graph(adj, n))).then_inc(adj_ld, 16)

            load_adj(0)
            pool.wait_ge(mask_ps, K)
            load_adj(1)
            with pool.Fori(2, Bn) as n:
                pool.wait_ge(mask_ps, n * K)
                load_adj(n)

        @block.tensor
        def _(pe):
            pe.wait_ge(consts, 4)

            def mask_transpose(n, k):
                if k == 0:
                    pe.wait_ge(adj_ld, (n + 1) * 16)
                    if not (isinstance(n, int) and n == 0):
                        pe.wait_ge(xf_done, n)
                else:
                    pe.wait_ge(mask_done, n * K + k)
                for t in range(T):
                    last = nc.tensor.transpose(fps[:, t * P:(t + 1) * P], adj_w[:, t, k * P:(k + 1) * P], ident[:, :])
                last.then_inc(mask_ps, 1)

            def h_transpose(n):
                pe.wait_ge(ln_done, n + 1)
                pe.wait_ge(mask_done, (n + 1) * K)
                for t in range(T):
                    last = nc.tensor.transpose(fps[:, t * P:(t + 1) * P], xn[:, t, :], ident[:, :])
                last.then_inc(hT_ps, 1)

            def scores(n):
                pe.wait_ge(hT_done, n + 1)
                if isinstance(n, int) and n == 0:
                    pe.wait_ge(ws_done, 1)
                else:
                    pe.wait_ge(summ_done, n * (T // 2))
                for t in range(T):
                    nc.tensor.matmul(mps[:, 0, t * 2 * H:(t + 1) * 2 * H], hT[:, t * P:(t + 1) * P], w_s[:, :],
                                     start=True, stop=True)
                pe.wait_ge(hrep_done, n + 1)
                nc.tensor.matmul(mps[:, 0, P:2 * P], hsum_rep[:, :], w_sb[:, :], start=True, stop=True).then_inc(s_ps, 1)
                for c in range(2):
                    last = nc.tensor.matmul(fps[0:2 * H, c * BANK:(c + 1) * BANK], w_s[:, :],
                                            hT[:, c * BANK:(c + 1) * BANK], start=True, stop=True)
                last.then_inc(sT_ps, 1)

            def max_and_values(n):
                pe.wait_ge(diag_done, n + 1)
                nc.tensor.matmul(mps[:, 1, 0:H], ones[:, :], smax_diag[:, :], start=True, stop=True).then_inc(m_ps, 1)
                for t in range(T):
                    last = nc.tensor.matmul(fps[:, t * F:(t + 1) * F], hT[:, t * P:(t + 1) * P], w_sb[:, :],
                                            start=True, stop=True)
                last.then_inc(wh_ps, 1)

            def head(b, p, h):
                n = b * H + h
                pe.wait_ge(g_done, n + 1)
                if h >= 2 or not (isinstance(b, int) and b == 0):
                    pe.wait_ge(sumg_done, n - 1)
                settle(pe)
                for t in range(T):
                    for j in range(T):
                        last = nc.tensor.matmul(acc[h % 2][:, t, 0:CP], g8[:, h % NG, j // R, t * P:(t + 1) * P, j % R],
                                                xp[p][:, j, h, :, :].rearrange("p a c -> p (a c)"),
                                                start=(j == 0), stop=(j == T - 1))
                last.then_inc(acc_done, 1)

            def mterm(b, p, q):
                if q:
                    pe.wait_ge(summ_done, b * (T // 2) + q)
                else:
                    pe.wait_ge(m_done, b + 1)
                settle(pe)
                for c in range(2):
                    t = 2 * q + c
                    for j in range(T):
                        last = nc.tensor.matmul(mps[:, c, 0:PARTS * H * V],
                                                mask8[p][:, j // R, t * P:(t + 1) * P, j % R],
                                                xp[p][:, j, :, :, V:C].rearrange("p h a c -> p a h c"),
                                                start=(j == 0), stop=(j == T - 1))
                last.then_inc(mterm_ps, 1)

            for k in range(K):
                mask_transpose(0, k)
            h_transpose(0)
            scores(0)
            max_and_values(0)

            def batch(b, p, front, post):
                pe.wait_ge(xp_done, b + 1)
                for h in range(H):
                    head(b, p, h)
                    if h < T // 2:
                        mterm(b, p, h)
                    if front:
                        if h < K:
                            mask_transpose(b + 1, h)
                        elif h == 3:
                            h_transpose(b + 1)
                        elif h == 4:
                            scores(b + 1)
                        elif h == 5:
                            max_and_values(b + 1)

            each_batch(pe, batch)

        @block.scalar
        def _(act):
            def gen(b, p, h):
                n = b * H + h
                first = isinstance(b, int) and b == 0
                act.wait_ge(s1bc_ld[h // 2], (b + 1) * 16)
                if not (first and h < NG):
                    act.wait_ge(acc_done, n - NG + 1)
                settle(act)
                for j in range(DVE_UNITS[h], T):
                    nc.scalar.activation(g8[:, h % NG, j // R, :, j % R], s1bc[:, h, :], ACT.Relu,
                                         bias=bigs2[p][:, j, h:h + 1], scale=BIG, saturate=False).then_inc(gen_act, 1)

            def ln_log(n):
                act.wait_ge(ln_mv, (n + 1) * (T + 1))
                nc.scalar.activation(rs_t[:, :], rs[:, :], ACT.Ln).then_inc(ln_ln, 1)
                act.wait_ge(ln_ln, n + 1)
                nc.scalar.activation(rs_t[:, :], rs_t[:, :], ACT.Exp, scale=-0.5).then_inc(ln_rs0, 1)

            def h_out(n):
                act.wait_ge(hT_ps, n + 1)
                nc.scalar.activation(hT[:, :], fps[:, :], ACT.Relu, accum_out=hsum[:, :]).then_inc(hT_done, 1)

            def h_rep(n):
                act.wait_ge(hT_done, n + 1)
                nc.scalar.activation(hsum_rep[:, :], hsum[:, :].broadcast_to([P, P]), ACT.Copy).then_inc(hrep_done, 1)

            def rows_out(n):
                act.wait_ge(sT_ps, n + 1)
                if not (isinstance(n, int) and n == 0):
                    act.wait_ge(s1_st, n * 16)
                nc.scalar.activation(sT[:, :], fps[0:H, :], ACT.Copy).then_inc(sT_done, 1)

            def exps(n, p):
                act.wait_ge(expo_step, (n + 1) * 4)
                nc.scalar.activation(bd[:, :, :, :], expo[:, 0:2, :, :], ACT.Exp).then_inc(exp_done, 1)
                nc.scalar.activation(rho[p][:, :, :], expo[:, 2, :, :], ACT.Exp).then_inc(exp_done, 1)

            def part(n, p, which, after, done):
                act.wait_ge(after, n + 1 if which else (n + 1) * 4)
                nc.scalar.activation(xp[p][:, :, :, which, :].rearrange("p t h c -> p (t h) c"), xf[:, :, :],
                                     ACT.Copy).then_inc(done, 1)

            def out_log(n):
                act.wait_ge(p_mv, (n + 1) * (T + 1))
                nc.scalar.activation(rs2_t[:, :], rs2[:, :], ACT.Ln).then_inc(p_ln, 1)
                act.wait_ge(p_ln, n + 1)
                nc.scalar.activation(rs2_t[:, :], rs2_t[:, :], ACT.Exp, scale=-0.5).then_inc(p_rs0, 1)

            def out_exp(n):
                act.wait_ge(p_z, n + 1)
                nc.scalar.activation(e_out[:, :, :], agg[:, :, :], ACT.Exp, bias=1.0).then_inc(p_exp, 1)

            ln_log(0)
            h_out(0)
            h_rep(0)
            rows_out(0)
            exps(0, 0)
            part(0, 0, 0, xf_done, hi_done)
            part(0, 0, 1, rest1, mid_done)
            act.wait_ge(thr_done, 2)
            gen(0, 0, 0)

            def batch(b, p, front, post):
                for h in range(H):
                    if post:
                        if h == 1:
                            out_log(b - 1)
                        if h == 2:
                            out_exp(b - 1)
                    if front:
                        if h == 3:
                            ln_log(b + 1)
                            h_out(b + 1)
                            h_rep(b + 1)
                        if h == 5:
                            rows_out(b + 1)
                        if h == 6:
                            exps(b + 1, 1 - p)
                            part(b + 1, 1 - p, 0, xf_done, hi_done)
                        if h == 7:
                            part(b + 1, 1 - p, 1, rest1, mid_done)
                            act.wait_ge(thr_done, (b + 2) * 2)
                            gen(b + 1, 1 - p, 0)
                    if h < H - 1:
                        gen(b, p, h + 1)

            each_batch(act, batch)
            out_log(Bn - 1)
            out_exp(Bn - 1)

        @block.vector
        def _(dve):
            v = nc.vector

            def newton(step, n, r, var, t2):
                v.tensor_tensor(t2, r, r, ALU.mult).then_inc(step, 1)
                dve.wait_ge(step, n * 4 + 1)
                v.tensor_tensor(t2, t2, var, ALU.mult).then_inc(step, 1)
                dve.wait_ge(step, n * 4 + 2)
                v.tensor_scalar(t2, t2, -0.5, 1.5, ALU.mult, ALU.add).then_inc(step, 1)
                dve.wait_ge(step, n * 4 + 3)
                v.tensor_tensor(r, r, t2, ALU.mult).then_inc(step, 1)
                dve.wait_ge(step, n * 4 + 4)

            def gen(b, p, h):
                n = b * H + h
                first = isinstance(b, int) and b == 0
                dve.wait_ge(s1bc_ld[h // 2], (b + 1) * 16)
                if not (first and h < NG):
                    dve.wait_ge(acc_done, n - NG + 1)
                settle(dve)
                for j in range(DVE_UNITS[h]):
                    v.tensor_scalar(g8[:, h % NG, j // R, :, j % R], s1bc[:, h, :], thr[p][:, j, h:h + 1], None,
                                    ALU.is_gt, saturate=False).then_inc(gen_dve, 1)

            def mask_g(b, p, h):
                dve.wait_ge(gen_act, b * ACT_G + sum(T - u for u in DVE_UNITS[:h + 1]))
                dve.wait_ge(gen_dve, b * DVE_G + sum(DVE_UNITS[:h + 1]))
                v.tensor_tensor(g[:, h % NG, :, :], g[:, h % NG, :, :], mask[p][:, :, :], ALU.bitwise_and).then_inc(g_done, 1)

            def sum_parts(b, p, h):
                dve.wait_ge(acc_done, b * H + h + 1)
                v.tensor_reduce(sumg[p][:, :, h, :], acc[h % 2][:, :, 0:CP].rearrange("p t (a c) -> p t c a", a=PARTS),
                                axis=AX.X, op=ALU.add).then_inc(sumg_done, 1)

            def sum_mterm(b, p, q):
                dve.wait_ge(mterm_ps, b * (T // 2) + q + 1)
                v.tensor_reduce(summ[p][:, 2 * q:2 * q + 2, :],
                                mps[:, :, 0:PARTS * H * V].rearrange("p t (a c) -> p t c a", a=PARTS),
                                axis=AX.X, op=ALU.add).then_inc(summ_done, 1)

            def mask_out(n, p, k):
                dve.wait_ge(mask_ps, n * K + k + 1)
                v.tensor_scalar(mask[p][:, k, :], fps[:, :].bitcast(U32), 3, None,
                                ALU.logical_shift_left).then_inc(mask_done, 1)

            def ln_in(n):
                dve.wait_ge(x_ln_ld, (n + 1) * 16)
                for t in range(T):
                    v.bn_stats(stats[:, t, :], x_ln[:, t, :]).then_inc(ln_stats, 1)
                dve.wait_ge(ln_stats, (n + 1) * T)
                settle(dve)
                for t in range(T):
                    v.bn_aggr(mv[:, t, :], stats[:, t, :]).then_inc(ln_mv, 1)
                dve.wait_ge(ln_mv, n * (T + 1) + T)
                v.tensor_scalar(rs[:, :], mv[:, :, 1], EPS, None, ALU.add).then_inc(ln_mv, 1)

            def ln_out(n):
                dve.wait_ge(ln_rs0, n + 1)
                newton(ln_newton, n, rs_t[:, :], rs[:, :], stats[:, :, 0])
                if not (isinstance(n, int) and n == 0):
                    dve.wait_ge(hT_ps, n)
                for t in range(T):
                    last = v.tensor_scalar(xn[:, t, :], x_ln[:, t, :], mv[:, t, 0:1], rs_t[:, t:t + 1],
                                           ALU.subtract, ALU.mult)
                last.then_inc(ln_done, 1)

            def keep_scores(n, p):
                dve.wait_ge(s_ps, n + 1)
                s = mps[:, 0, 0:2 * H * T].rearrange("p (t c) -> p t c", t=T)
                v.tensor_tensor(s2n[:, :, :], s[:, :, H:2 * H],
                                edge[:, :].rearrange("p (a h) -> p a h", a=1).broadcast_to([P, T, H]), ALU.add).then_inc(s_kept, 1)
                v.tensor_copy(s1n[:, :, :], s[:, :, 0:H]).then_inc(s_kept, 1)
                v.tensor_copy(wsum[p][:, :, 0:DH], mps[:, 0, P:2 * P].rearrange("p (h c) -> p h c", h=H)).then_inc(wsum_done, 1)
                dve.wait_ge(s_kept, (n + 1) * 2)
                v.tensor_scalar(thr[p][:, :, :], s2n[:, :, :], -1.0, None, ALU.mult).then_inc(thr_done, 1)
                v.tensor_scalar(bigs2[p][:, :, :], s2n[:, :, :], BIG, None, ALU.mult).then_inc(thr_done, 1)

            def row_max(n):
                dve.wait_ge(sT_done, n + 1)
                v.reduce_max(smax[:, :], fps[0:2 * H, :], axis=AX.X).then_inc(smax_done, 1)
                dve.wait_ge(smax_done, n + 1)
                v.tensor_scalar(smax_diag[:, :], ident[0:2 * H, H:2 * H], smax[:, 0:1], None, ALU.mult).then_inc(diag_done, 1)

            def exponents(n):
                dve.wait_ge(m_ps, n + 1)
                v.tensor_tensor(m_bc[:, :], mps[:, 1, 0:H], edge[:, :], ALU.add).then_inc(m_done, 1)
                dve.wait_ge(m_done, n + 1)
                m = m_bc[:, :].rearrange("p (a h) -> p a h", a=1).broadcast_to([P, T, H])
                if not (isinstance(n, int) and n == 0):
                    dve.wait_ge(exp_done, n * 2)
                v.tensor_tensor(expo[:, 0, :, :], s2n[:, :, :], m, ALU.subtract).then_inc(expo_step, 1)
                v.tensor_tensor(expo[:, 2, :, :], s1n[:, :, :], m, ALU.add).then_inc(expo_step, 1)
                dve.wait_ge(expo_step, n * 4 + 2)
                v.tensor_scalar(expo[:, 1, :, :], expo[:, 0, :, :], SLOPE, None, ALU.mult).then_inc(expo_step, 1)
                v.tensor_scalar(expo[:, 2, :, :], expo[:, 2, :, :], RHO_CAP, 1.0 - SLOPE, ALU.min, ALU.mult).then_inc(expo_step, 1)

            def values(n):
                dve.wait_ge(wh_ps, n + 1)
                if not (isinstance(n, int) and n == 0):
                    dve.wait_ge(xp_done, n)
                dve.wait_ge(exp_done, n * 2 + 2)
                wh = fps[:, :].rearrange("p (q c) -> p q c", c=DH)
                for c in range(2):
                    f = bd[:, c, :, :].rearrange("p t (h a) -> p (t h) a", a=1)
                    v.tensor_tensor(xf[:, :, c * V:c * V + DH], wh, f.broadcast_to([P, T * H, DH]), ALU.mult).then_inc(xf_step, 1)
                    last = v.tensor_copy(xf[:, :, c * V + DH:(c + 1) * V], f)
                    last.then_inc(xf_done, 1) if False else last.then_inc(xf_step, 1)

            def split1(n, p):
                dve.wait_ge(hi_done, n + 1)
                v.tensor_tensor(xf[:, :, :], xf[:, :, :], xp[p][:, :, :, 0, :].rearrange("p t h c -> p (t h) c"),
                                ALU.subtract).then_inc(rest1, 1)

            def split2(n, p):
                dve.wait_ge(mid_done, n + 1)
                v.tensor_tensor(xp[p][:, :, :, 2, :].rearrange("p t h c -> p (t h) c"), xf[:, :, :],
                                xp[p][:, :, :, 1, :].rearrange("p t h c -> p (t h) c"), ALU.subtract).then_inc(xp_done, 1)

            def combine(n, p):
                dve.wait_ge(sumg_done, (n + 1) * H)
                dve.wait_ge(summ_done, (n + 1) * (T // 2))
                sg = sumg[p][:, :, :, :].rearrange("p t h c -> p (t h) c")
                sm = summ[p][:, :, :].rearrange("p t (h c) -> p (t h) c", c=V)
                r = rho[p][:, :, :].rearrange("p t (h a) -> p (t h) a", a=1).broadcast_to([P, T * H, V])
                v.tensor_scalar(lone[:, :], summ[p][:, :, DH], 0.0, None, ALU.is_equal).then_inc(p_lone, 1)
                v.tensor_tensor(num[:, :, :], sg[:, :, 0:V], r, ALU.mult).then_inc(p_rho, 1)
                dve.wait_ge(p_lone, n + 1)
                v.tensor_tensor(sm, sm, sg[:, :, V:C], ALU.subtract).then_inc(p_sub, 1)
                dve.wait_ge(p_rho, n + 1)
                dve.wait_ge(p_sub, n + 1)
                v.tensor_tensor(num[:, :, :], num[:, :, :], sm, ALU.add).then_inc(p_add, 1)
                dve.wait_ge(p_add, n + 1)
                nt = num[:, :, :].rearrange("p (t h) c -> p t (h c)", t=T)
                for t in range(T):
                    v.scalar_tensor_tensor(nt[:, t, :], wsum[p][:, :, :].rearrange("p h c -> p (h c)"), lone[:, t:t + 1],
                                           nt[:, t, :], ALU.mult, ALU.add).then_inc(p_fix, 1)
                dve.wait_ge(p_fix, (n + 1) * T)
                v.reciprocal(rden[:, :], num[:, :, DH]).then_inc(p_rden, 1)
                dve.wait_ge(p_rden, n + 1)
                v.tensor_tensor(agg[:, :, :].rearrange("p t (h c) -> p (t h) c", c=DH), num[:, :, 0:DH],
                                rden[:, :].rearrange("p (q a) -> p q a", a=1).broadcast_to([P, T * H, DH]),
                                ALU.mult).then_inc(p_agg, 1)

            def out_stats(n):
                dve.wait_ge(p_agg, n + 1)
                for t in range(T):
                    v.bn_stats(stats2[:, t, :], agg[:, t, :]).then_inc(p_stats, 1)
                dve.wait_ge(p_stats, (n + 1) * T)
                settle(dve)
                for t in range(T):
                    v.bn_aggr(mv2[:, t, :], stats2[:, t, :]).then_inc(p_mv, 1)
                dve.wait_ge(p_mv, n * (T + 1) + T)
                v.tensor_scalar(rs2[:, :], mv2[:, :, 1], EPS, None, ALU.add).then_inc(p_mv, 1)

            def out_norm(n):
                dve.wait_ge(p_rs0, n + 1)
                newton(p_newton, n, rs2_t[:, :], rs2[:, :], stats2[:, :, 0])
                for t in range(T):
                    v.tensor_scalar(agg[:, t, :], agg[:, t, :], mv2[:, t, 0:1], rs2_t[:, t:t + 1],
                                    ALU.subtract, ALU.mult).then_inc(p_norm, 1)
                dve.wait_ge(p_norm, (n + 1) * T)
                gb = [c[:, :].rearrange("p (a f) -> p a f", a=1).broadcast_to([P, T, F]) for c in (gam, bet)]
                v.tensor_tensor(agg[:, :, :], agg[:, :, :], gb[0], ALU.mult).then_inc(p_gam, 1)
                dve.wait_ge(p_gam, n + 1)
                v.tensor_tensor(agg[:, :, :], agg[:, :, :], gb[1], ALU.add).then_inc(p_z, 1)

            def out_elu(n):
                dve.wait_ge(p_z, n + 1)
                dve.wait_ge(x_res_ld, (n + 1) * 16)
                if not (isinstance(n, int) and n == 0):
                    dve.wait_ge(out_st, n * 16)
                v.scalar_tensor_tensor(y[:, :, :], agg[:, :, :], -1.0, x_res[:, :, :], ALU.max, ALU.add).then_inc(p_y, 1)
                dve.wait_ge(p_y, n + 1)
                dve.wait_ge(p_exp, n + 1)
                v.scalar_tensor_tensor(y[:, :, :], e_out[:, :, :], 1.0, y[:, :, :], ALU.min, ALU.add).then_inc(p_out, 1)

            xf_step = xf_done

            dve.wait_ge(const_ld, 6 * 16)
            for c in range(2):
                v.tensor_tensor(wa_prod[:, c, :].rearrange("p (h d) -> p h d", h=H),
                                w_sb[:, :].rearrange("p (h d) -> p h d", h=H),
                                a12[:, c:c + 1, :].broadcast_to([P, H, DH]), ALU.mult).then_inc(ws_prod, 1)
            dve.wait_ge(ws_prod, 2)
            v.tensor_reduce(w_s[:, :], wa_prod[:, :, :].rearrange("p c (h d) -> p (c h) d", h=H), axis=AX.X,
                            op=ALU.add).then_inc(ws_done, 1)
            v.tensor_scalar(bet[:, :], bet[:, :], -1.0, None, ALU.add).then_inc(ws_done, 1)
            dve.wait_ge(ws_done, 2)
            ln_in(0)
            for k in range(K):
                mask_out(0, 0, k)
            ln_out(0)
            keep_scores(0, 0)
            row_max(0)
            exponents(0)
            values(0)
            split1(0, 0)
            split2(0, 0)
            gen(0, 0, 0)

            def batch(b, p, front, post):
                for h in range(H):
                    if h < H - 1:
                        gen(b, p, h + 1)
                    mask_g(b, p, h)
                    if h:
                        sum_parts(b, p, h - 1)
                    if 0 < h <= T // 2:
                        sum_mterm(b, p, h - 1)
                    if front and h < K + 1 and h:
                        mask_out(b + 1, 1 - p, h - 1)
                    if post:
                        if h == 0:
                            combine(b - 1, 1 - p)
                            out_stats(b - 1)
                        if h == 1:
                            out_norm(b - 1)
                        if h == 3:
                            out_elu(b - 1)
                    if front:
                        if h == 2:
                            ln_in(b + 1)
                        if h == 3:
                            ln_out(b + 1)
                        if h == 5:
                            keep_scores(b + 1, 1 - p)
                            row_max(b + 1)
                        if h == 6:
                            exponents(b + 1)
                            values(b + 1)
                        if h == 7:
                            split1(b + 1, 1 - p)
                            split2(b + 1, 1 - p)
                            gen(b + 1, 1 - p, 0)
                sum_parts(b, p, H - 1)

            each_batch(dve, batch)
            combine(Bn - 1, 1)
            out_stats(Bn - 1)
            out_norm(Bn - 1)
            out_elu(Bn - 1)


_INS = ['x', 'adj', 'L0_gnn_W', 'L0_gnn_a1', 'L0_gnn_a2', 'L0_gnn_edge_emb', 'L0_gnn_ln_gamma', 'L0_gnn_ln_beta']


def kernel(**inputs):
    import concourse.bacc as _bacc
    from concourse.bass_utils import run_bass_kernel_spmd as _run

    nc = _bacc.Bacc("TRN2", target_bir_lowering=False, num_devices=1)
    arrays, args = {}, []
    for name in _INS:
        a = np.ascontiguousarray(inputs[name])
        arrays[f"in_{name}_dram"] = a
        args.append(nc.dram_tensor(f"in_{name}_dram", a.shape, mybir.dt.from_np(a.dtype), kind="ExternalInput").ap())
    o = nc.dram_tensor("out_0_dram", inputs['x'].shape, F32, kind="ExternalOutput").ap()
    gat_block(nc, *args, o)
    r = _run(nc, [arrays], core_ids=[0])
    return r.results[0]["out_0_dram"]
```

```python
import numpy as np
import concourse.bass as bass
from concourse import mybir
from contextlib import ExitStack

F32 = mybir.dt.float32
BF16 = mybir.dt.bfloat16
FP8 = mybir.dt.float8e4
U32 = mybir.dt.uint32
U8 = mybir.dt.uint8
ALU = mybir.AluOpType
ACT = mybir.ActivationFunctionType
AX = mybir.AxisListType


def gat_block(nc, x, adj, W, a1, a2, edge_emb, gamma, beta, out):
    Bn, N, F = x.shape
    H = edge_emb.shape[1]
    DH = F // H
    P = 128
    T = N // P
    R = 4
    K = T // R
    V = DH + 1
    C = 2 * V
    PARTS = 3
    CP = PARTS * C
    PITCH = 128
    BANK = 512
    NG = 4
    SLOPE = 0.2
    EPS = 1e-5
    BIG = float(2 ** 60)
    RHO_CAP = 100.0
    FIRST = [3, 1, 2, 2, 2, 2, 1, 1]
    MID = [1, 1, 1, 1, 0, 1, 0, 1]
    LAST = [1, 1, 2, 2, 2, 2, 2, 2]
    assert LAST[:2] == MID[:2]

    def dve_tiles(b):
        return (FIRST if b == 0 else LAST if b == Bn - 1 else MID) if isinstance(b, int) else MID

    def act_tiles(b):
        return [T - u for u in dve_tiles(b)]

    def count(tiles, b, h):
        if isinstance(b, int) and b == 0:
            return sum(tiles(0)[:h + 1])
        return sum(tiles(0)) + (b - 1) * sum(tiles(1)) + sum(tiles(b)[:h + 1])

    s1_rows = nc.dram_tensor("s1_rows", (2, H, N), F32, kind="Internal").ap()

    ctx = ExitStack()
    with ctx:
        def sb(name, shape, dt):
            return ctx.enter_context(nc.sbuf_tensor(name, shape, dt))

        def pb(name, shape, dt):
            return ctx.enter_context(nc.psum_tensor(name, shape, dt))

        def sem(name):
            return ctx.enter_context(nc.semaphore(name))

        ident = sb("ident", [P, P], F32)
        ones = sb("ones", [2 * H, P], F32)
        minus_half = sb("minus_half", [P, T], F32)
        w_sb = sb("w_sb", [P, F], F32)
        a12 = sb("a12", [P, 2, DH], F32)
        wa_prod = sb("wa_prod", [P, 2, F], F32)
        w_s = sb("w_s", [P, 2 * H], F32)
        edge = sb("edge", [P, H], F32)
        gam = sb("gam", [P, F], F32)
        bet = sb("bet", [P, F], F32)
        x_ln = sb("x_ln", [P, T, F], F32)
        x_res = sb("x_res", [P, T, F], F32)
        stats = sb("stats", [P, T, 6], F32)
        mv = sb("mv", [P, T, 2], F32)
        var = sb("var", [P, T], F32)
        rs = sb("rs", [P, T], F32)
        xn = sb("xn", [P, T, F], F32)
        hT = sb("hT", [P, N], F32)
        hsum = sb("hsum", [P, 1], F32)
        hsum_rep = sb("hsum_rep", [P, P], F32)
        sn = sb("sn", [P, T, 2 * H], F32)
        thr = [sb(f"thr{p}", [P, T, H], F32) for p in range(2)]
        bigs2 = [sb(f"bigs2{p}", [P, T, H], F32) for p in range(2)]
        wsum = [sb(f"wsum{p}", [P, H, V], F32) for p in range(2)]
        sT = sb("sT", [H, N], F32)
        smax = sb("smax", [2 * H, 1], F32)
        smax_diag = sb("smax_diag", [2 * H, H], F32)
        m_bc = sb("m_bc", [P, H], F32)
        expo = sb("expo", [P, 3, T, H], F32)
        bd = sb("bd", [P, 2, T, H], F32)
        rho = [sb(f"rho{p}", [P, T, H], F32) for p in range(2)]
        s1bc = sb("s1bc", [P, H, N], F32)
        xp = [sb(f"xp{p}", [P, T, H, PARTS, C], F32) for p in range(2)]
        adj8 = sb("adj8", [P, T, N], U8)
        mask = [sb(f"mask{p}", [P, K, N], U32) for p in range(2)]
        g = sb("g", [P, NG, K, N], U32)
        sumg = [sb(f"sumg{p}", [P, T, H, C], F32) for p in range(2)]
        summ = [sb(f"summ{p}", [P, T, H * V], F32) for p in range(2)]
        lone = sb("lone", [P, T], F32)
        num = sb("num", [P, T * H, V], F32)
        rden = sb("rden", [P, T * H], F32)
        agg = sb("agg", [P, T, F], F32)
        stats2 = sb("stats2", [P, T, 6], F32)
        mv2 = sb("mv2", [P, T, 2], F32)
        var2 = sb("var2", [P, T], F32)
        rs2 = sb("rs2", [P, T], F32)
        e_out = sb("e_out", [P, T, F], F32)

        acc = [pb(f"acc{q}", [P, T, PITCH], F32) for q in range(2)]
        mps = pb("mps", [P, 2, BANK], F32)
        fps = pb("fps", [P, 2 * BANK], F32)

        mps_flat = mps[:, :, :].rearrange("p a c -> p (a c)")
        g8 = g[:, :, :, :].bitcast(FP8).rearrange("p n k (i r) -> p n k i r", r=R)
        mask8 = [m[:, :, :].bitcast(FP8).rearrange("p k (i r) -> p k i r", r=R) for m in mask]
        xp16 = [q[:, :, :, :, :].bitcast(BF16).rearrange("p t h a (c w) -> p t h a c w", w=2)[:, :, :, :, :, 1]
                for q in xp]
        adj_w = adj8[:, :, :].bitcast(F32)

        const_ld = sem("const_ld")
        x_ln_ld = sem("x_ln_ld")
        x_res_ld = sem("x_res_ld")
        adj_ld = sem("adj_ld")
        s1_st = sem("s1_st")
        s1bc_ld = [sem(f"s1bc_ld{q}") for q in range(H // 2)]
        out_st = sem("out_st")
        ident_zero = sem("ident_zero")
        consts = sem("consts")
        waits_met = sem("waits_met")
        ws_prod = sem("ws_prod")
        ws_done = sem("ws_done")
        ln_stats = sem("ln_stats")
        ln_mv = sem("ln_mv")
        ln_var = sem("ln_var")
        ln_rs = sem("ln_rs")
        ln_done = sem("ln_done")
        hT_ps = sem("hT_ps")
        hT_done = sem("hT_done")
        hrep_done = sem("hrep_done")
        s_ps = sem("s_ps")
        sT_ps = sem("sT_ps")
        s_kept = sem("s_kept")
        thr_done = sem("thr_done")
        wsum_done = sem("wsum_done")
        sT_done = sem("sT_done")
        smax_done = sem("smax_done")
        diag_done = sem("diag_done")
        m_ps = sem("m_ps")
        m_done = sem("m_done")
        expo_step = sem("expo_step")
        exp_done = sem("exp_done")
        wh_ps = sem("wh_ps")
        values_done = sem("values_done")
        rest1 = sem("rest1")
        xp_done = sem("xp_done")
        mask_ps = sem("mask_ps")
        mask_done = sem("mask_done")
        gen_act = sem("gen_act")
        gen_dve = sem("gen_dve")
        g_done = sem("g_done")
        acc_done = sem("acc_done")
        sumg_done = sem("sumg_done")
        mterm_ps = sem("mterm_ps")
        summ_done = sem("summ_done")
        p_sub = sem("p_sub")
        p_lone = sem("p_lone")
        p_rho = sem("p_rho")
        p_add = sem("p_add")
        p_fix = sem("p_fix")
        p_rden = sem("p_rden")
        p_agg = sem("p_agg")
        p_stats = sem("p_stats")
        p_mv = sem("p_mv")
        p_var = sem("p_var")
        p_rs = sem("p_rs")
        p_gam = sem("p_gam")
        p_z = sem("p_z")
        p_exp = sem("p_exp")
        p_y = sem("p_y")
        p_out = sem("p_out")

        def nodes(ap2d):
            return ap2d.rearrange("(k p r) f -> p k r f", k=K, p=P)

        def tiles(t):
            return t.rearrange("p (k r) f -> p k r f", k=K)

        def graph(ap, b):
            return ap[b, :, :] if isinstance(b, int) else ap[bass.ds(b, 1), :, :].rearrange("a n f -> (a n) f")

        block = ctx.enter_context(nc.Block())

        def settle(eng):
            eng.sem_inc(waits_met, 1)

        def is_zero(n):
            return isinstance(n, int) and n == 0

        def each_batch(eng, batch):
            batch(0, 0, True, False)
            with eng.Fori(0, Bn // 2 - 1) as i:
                batch(i * 2 + 1, 1, True, True)
                batch(i * 2 + 2, 0, True, True)
            batch(Bn - 1, 1, False, True)

        @block.sync
        def _(sp):
            sp.dma_start(x_ln[:, :, :].rearrange("p (k r) f -> p k r f", k=K), nodes(x[0, :, :])).then_inc(x_ln_ld, 16)
            sp.dma_start(w_sb[:, :], W).then_inc(const_ld, 16)
            for c, v in enumerate((a1, a2)):
                sp.dma_start(a12[:, c, :], v.rearrange("(a d) -> a d", a=1).broadcast_to([P, DH])).then_inc(const_ld, 16)
            sp.dma_start(edge[:, :], edge_emb[1:2, :].broadcast_to([P, H])).then_inc(const_ld, 16)
            for t_, v in ((gam, gamma), (bet, beta)):
                sp.dma_start(t_[:, :], v.rearrange("(a d) -> a d", a=1).broadcast_to([P, F])).then_inc(const_ld, 16)

            def scores_out(n, p):
                sp.wait_ge(sT_done, n + 1)
                sp.dma_start(s1_rows[p, :, :], sT[:, :]).then_inc(s1_st, 16)
                sp.wait_ge(s1_st, (n + 1) * 16)
                for q in range(H // 2):
                    if not is_zero(n):
                        sp.wait_ge(gen_act, count(act_tiles, n - 1, 2 * q + 1))
                        settle(sp)
                        sp.wait_ge(gen_dve, count(dve_tiles, n - 1, 2 * q + 1))
                        settle(sp)
                    sp.dma_start(s1bc[:, 2 * q:2 * q + 2, :],
                                 s1_rows[p:p + 1, 2 * q:2 * q + 2, :].broadcast_to([P, 2, N])).then_inc(s1bc_ld[q], 16)

            def load_x_ln(n):
                sp.wait_ge(ln_done, n)
                sp.dma_start(tiles(x_ln[:, :, :]), nodes(graph(x, n))).then_inc(x_ln_ld, 16)

            def store_out(n):
                sp.wait_ge(p_out, n + 1)
                sp.dma_start(nodes(graph(out, n)), tiles(x_res[:, :, :])).then_inc(out_st, 16)

            def load_x_res(n):
                if not is_zero(n):
                    sp.wait_ge(out_st, n * 16)
                sp.dma_start(tiles(x_res[:, :, :]), nodes(graph(x, n))).then_inc(x_res_ld, 16)

            scores_out(0, 0)

            def batch(b, p, front, post):
                if front:
                    load_x_ln(b + 1)
                    scores_out(b + 1, 1 - p)
                if post:
                    store_out(b - 1)
                load_x_res(b)

            each_batch(sp, batch)
            store_out(Bn - 1)
            sp.wait_ge(out_st, Bn * 16)

        @block.gpsimd
        def _(pool):
            pool.memset(ident[:, :], 0.0).then_inc(ident_zero, 1)
            pool.memset(ones[:, :], 1.0).then_inc(consts, 1)
            pool.memset(minus_half[:, :], -0.5).then_inc(consts, 1)
            pool.wait_ge(ident_zero, 1)
            pool.affine_select(out=ident[:, :], in_=ident[:, :], compare_op=ALU.not_equal, fill=1.0, base=0,
                               pattern=[[-1, P]], channel_multiplier=1).then_inc(consts, 1)
            for w in wsum:
                pool.memset(w[:, :, DH:V], float(N)).then_inc(consts, 1)

            def load_adj(n):
                pool.dma_start(tiles(adj8[:, :, :]), nodes(graph(adj, n))).then_inc(adj_ld, 16)

            def inverse_roots(n, var_done, var_, rs_, done):
                pool.wait_ge(var_done, n + 1)
                pool.tensor_tensor(rs_[:, :], var_[:, :], minus_half[:, :], ALU.pow).then_inc(done, 1)

            load_adj(0)
            pool.wait_ge(consts, 5)
            inverse_roots(0, ln_var, var, rs, ln_rs)

            def batch(b, p, front, post):
                if front:
                    pool.wait_ge(mask_ps, (b + 1) * K)
                    load_adj(b + 1)
                if front:
                    inverse_roots(b + 1, ln_var, var, rs, ln_rs)
                if post:
                    inverse_roots(b - 1, p_var, var2, rs2, p_rs)

            each_batch(pool, batch)
            inverse_roots(Bn - 1, p_var, var2, rs2, p_rs)

        @block.tensor
        def _(pe):
            pe.wait_ge(consts, 5)

            def mask_transpose(n, k):
                if k:
                    pe.wait_ge(mask_done, n * K + k)
                else:
                    pe.wait_ge(adj_ld, (n + 1) * 16)
                    if not is_zero(n):
                        pe.wait_ge(summ_done, n * (T // 2))
                for t in range(T):
                    last = nc.tensor.transpose(mps_flat[:, t * P:(t + 1) * P], adj_w[:, t, k * P:(k + 1) * P], ident[:, :])
                last.then_inc(mask_ps, 1)

            def h_transpose(n):
                pe.wait_ge(ln_done, n + 1)
                if not is_zero(n):
                    pe.wait_ge(values_done, n * 4)
                for t in range(T):
                    last = nc.tensor.transpose(fps[:, t * P:(t + 1) * P], xn[:, t, :], ident[:, :])
                last.then_inc(hT_ps, 1)

            def scores(n):
                pe.wait_ge(hT_done, n + 1)
                if is_zero(n):
                    pe.wait_ge(ws_done, 2)
                for t in range(T):
                    nc.tensor.matmul(fps[:, t * 2 * H:(t + 1) * 2 * H], hT[:, t * P:(t + 1) * P], w_s[:, :],
                                     start=True, stop=True)
                pe.wait_ge(hrep_done, n + 1)
                nc.tensor.matmul(fps[:, P:2 * P], hsum_rep[:, :], w_sb[:, :], start=True, stop=True).then_inc(s_ps, 1)

            def scores_by_row(n):
                pe.wait_ge(s_kept, (n + 1) * 2)
                pe.wait_ge(wsum_done, n + 1)
                for t in range(T):
                    last = nc.tensor.transpose(fps[0:2 * H, t * P:(t + 1) * P], sn[:, t, :], ident[:, :])
                last.then_inc(sT_ps, 1)

            def largest(n):
                pe.wait_ge(diag_done, n + 1)
                nc.tensor.matmul(fps[:, 0:H], ones[:, :], smax_diag[:, :], start=True, stop=True).then_inc(m_ps, 1)

            def node_values(n):
                pe.wait_ge(m_done, n + 1)
                for t in range(T):
                    last = nc.tensor.matmul(fps[:, t * F:(t + 1) * F], hT[:, t * P:(t + 1) * P], w_sb[:, :],
                                            start=True, stop=True)
                last.then_inc(wh_ps, 1)

            def head(b, p, h):
                n = b * H + h
                pe.wait_ge(g_done, n + 1)
                if h >= 2 or not is_zero(b):
                    pe.wait_ge(sumg_done, n - 1)
                settle(pe)
                for t in range(T):
                    for j in range(T):
                        last = nc.tensor.matmul(acc[h % 2][:, t, 0:CP].rearrange("p (a c) -> p a c", a=PARTS),
                                                g8[:, h % NG, j // R, t * P:(t + 1) * P, j % R],
                                                xp16[p][:, j, h, :, :],
                                                start=(j == 0), stop=(j == T - 1))
                last.then_inc(acc_done, 1)

            def mterm(b, p, q):
                if q:
                    pe.wait_ge(summ_done, b * (T // 2) + q)
                else:
                    pe.wait_ge(mask_done, (b + 1) * K)
                settle(pe)
                for c in range(2):
                    t = 2 * q + c
                    for j in range(T):
                        last = nc.tensor.matmul(mps[:, c, 0:PARTS * H * V],
                                                mask8[p][:, j // R, t * P:(t + 1) * P, j % R],
                                                xp16[p][:, j, :, :, V:C].rearrange("p h a c -> p a h c"),
                                                start=(j == 0), stop=(j == T - 1))
                last.then_inc(mterm_ps, 1)

            h_transpose(0)
            mask_transpose(0, 0)
            scores(0)
            scores_by_row(0)
            mask_transpose(0, 1)
            largest(0)
            node_values(0)

            def batch(b, p, front, post):
                pe.wait_ge(xp_done, b + 1)
                for h in range(H):
                    head(b, p, h)
                    if front:
                        if h == 0:
                            h_transpose(b + 1)
                        elif h == 1:
                            scores(b + 1)
                        elif h == 2:
                            scores_by_row(b + 1)
                        elif h == 4:
                            largest(b + 1)
                            mask_transpose(b + 1, 0)
                        elif h == 5:
                            node_values(b + 1)
                        elif h == 6:
                            mask_transpose(b + 1, 1)
                    if h < T // 2:
                        mterm(b, p, h)

            each_batch(pe, batch)

        @block.scalar
        def _(act):
            def gen(b, p, h, between=None):
                n = b * H + h
                first = isinstance(b, int) and b == 0
                act.wait_ge(s1bc_ld[h // 2], (b + 1) * 16)
                if h == 0:
                    act.wait_ge(thr_done, (b + 1) * 2)
                if not (first and h < NG):
                    act.wait_ge(acc_done, n - NG + 1)
                settle(act)
                for j in range(dve_tiles(b)[h], T):
                    if between and j == T // 2:
                        between()
                        settle(act)
                    nc.scalar.activation(g8[:, h % NG, j // R, :, j % R], s1bc[:, h, :], ACT.Relu,
                                         bias=bigs2[p][:, j, h:h + 1], scale=BIG, saturate=False).then_inc(gen_act, 1)

            def h_out(n):
                act.wait_ge(hT_ps, n + 1)
                nc.scalar.activation(hT[:, :], fps[:, :], ACT.Relu, accum_out=hsum[:, :]).then_inc(hT_done, 1)

            def h_rep(n):
                act.wait_ge(hT_done, n + 1)
                nc.scalar.activation(hsum_rep[:, :], hsum[:, :].broadcast_to([P, P]), ACT.Copy).then_inc(hrep_done, 1)

            def rows_out(n):
                act.wait_ge(sT_ps, n + 1)
                if not is_zero(n):
                    act.wait_ge(s1_st, n * 16)
                nc.scalar.activation(sT[:, :], fps[0:H, :], ACT.Copy).then_inc(sT_done, 1)

            def exps(n, p):
                act.wait_ge(expo_step, (n + 1) * 4)
                nc.scalar.activation(bd[:, :, :, :], expo[:, 0:2, :, :], ACT.Exp).then_inc(exp_done, 1)
                nc.scalar.activation(rho[p][:, :, :], expo[:, 2, :, :], ACT.Exp).then_inc(exp_done, 1)

            def out_exp(n):
                act.wait_ge(p_z, (n + 1) * T)
                nc.scalar.activation(e_out[:, :, :], agg[:, :, :], ACT.Exp, bias=1.0).then_inc(p_exp, 1)

            h_out(0)
            h_rep(0)
            rows_out(0)
            exps(0, 0)
            gen(0, 0, 0)
            gen(0, 0, 1)

            def batch(b, p, front, post):
                for h in range(H):
                    step = None
                    if front and h == 1:
                        step = lambda: (h_out(b + 1), h_rep(b + 1))
                    if front and h == 3:
                        step = lambda: rows_out(b + 1)
                    if post and h == 4:
                        step = lambda: out_exp(b - 1)
                    if front and h == 5:
                        exps(b + 1, 1 - p)
                    if h < H - 2:
                        gen(b, p, h + 2, step)
                    elif front:
                        gen(b + 1, 1 - p, h + 2 - H, step)

            each_batch(act, batch)
            out_exp(Bn - 1)

        @block.vector
        def _(dve):
            v = nc.vector

            def gen(b, p, h):
                n = b * H + h
                first = isinstance(b, int) and b == 0
                dve.wait_ge(s1bc_ld[h // 2], (b + 1) * 16)
                if not (first and h < NG):
                    dve.wait_ge(acc_done, n - NG + 1)
                settle(dve)
                for j in range(dve_tiles(b)[h]):
                    v.tensor_scalar(g8[:, h % NG, j // R, :, j % R], s1bc[:, h, :], thr[p][:, j, h:h + 1], None,
                                    ALU.is_gt, saturate=False).then_inc(gen_dve, 1)

            def mask_g(b, p, h):
                dve.wait_ge(gen_act, count(act_tiles, b, h))
                dve.wait_ge(gen_dve, count(dve_tiles, b, h))
                if h == 0:
                    dve.wait_ge(mask_done, (b + 1) * K)
                v.tensor_tensor(g[:, h % NG, :, :], g[:, h % NG, :, :], mask[p][:, :, :], ALU.bitwise_and).then_inc(g_done, 1)

            def sum_parts(b, p, h):
                dve.wait_ge(acc_done, b * H + h + 1)
                v.tensor_reduce(sumg[p][:, :, h, :], acc[h % 2][:, :, 0:CP].rearrange("p t (a c) -> p t c a", a=PARTS),
                                axis=AX.X, op=ALU.add).then_inc(sumg_done, 1)

            def sum_mterm(b, p, q):
                dve.wait_ge(mterm_ps, b * (T // 2) + q + 1)
                v.tensor_reduce(summ[p][:, 2 * q:2 * q + 2, :],
                                mps[:, :, 0:PARTS * H * V].rearrange("p t (a c) -> p t c a", a=PARTS),
                                axis=AX.X, op=ALU.add).then_inc(summ_done, 1)

            def mask_out(n, p, k):
                dve.wait_ge(mask_ps, n * K + k + 1)
                v.tensor_scalar(mask[p][:, k, :], mps_flat.bitcast(U32), 3, None,
                                ALU.logical_shift_left).then_inc(mask_done, 1)

            def ln_in(n):
                dve.wait_ge(x_ln_ld, (n + 1) * 16)
                for t in range(T):
                    v.bn_stats(stats[:, t, :], x_ln[:, t, :]).then_inc(ln_stats, 1)
                dve.wait_ge(ln_stats, (n + 1) * T)
                settle(dve)
                for t in range(T):
                    v.bn_aggr(mv[:, t, :], stats[:, t, :]).then_inc(ln_mv, 1)
                dve.wait_ge(ln_mv, (n + 1) * T)
                v.tensor_scalar(var[:, :], mv[:, :, 1], EPS, None, ALU.add).then_inc(ln_var, 1)

            def ln_out(n):
                dve.wait_ge(ln_rs, n + 1)
                if not is_zero(n):
                    dve.wait_ge(hT_ps, n)
                for t in range(T):
                    last = v.tensor_scalar(xn[:, t, :], x_ln[:, t, :], mv[:, t, 0:1], rs[:, t:t + 1],
                                           ALU.subtract, ALU.mult)
                last.then_inc(ln_done, 1)

            def keep_scores(n, p):
                dve.wait_ge(s_ps, n + 1)
                if not (isinstance(n, int) and n < 2):
                    dve.wait_ge(p_fix, (n - 1) * T)
                s = fps[:, 0:2 * H * T].rearrange("p (t c) -> p t c", t=T)
                v.tensor_tensor(sn[:, :, H:2 * H], s[:, :, H:2 * H],
                                edge[:, :].rearrange("p (a h) -> p a h", a=1).broadcast_to([P, T, H]), ALU.add).then_inc(s_kept, 1)
                v.tensor_copy(sn[:, :, 0:H], s[:, :, 0:H]).then_inc(s_kept, 1)
                v.tensor_copy(wsum[p][:, :, 0:DH], fps[:, P:2 * P].rearrange("p (h c) -> p h c", h=H)).then_inc(wsum_done, 1)
                dve.wait_ge(s_kept, (n + 1) * 2)
                v.tensor_scalar(thr[p][:, :, :], sn[:, :, H:2 * H], -1.0, None, ALU.mult).then_inc(thr_done, 1)
                v.tensor_scalar(bigs2[p][:, :, :], sn[:, :, H:2 * H], BIG, None, ALU.mult).then_inc(thr_done, 1)

            def row_max(n):
                dve.wait_ge(sT_done, n + 1)
                v.reduce_max(smax[:, :], fps[0:2 * H, :], axis=AX.X).then_inc(smax_done, 1)
                dve.wait_ge(smax_done, n + 1)
                v.tensor_scalar(smax_diag[:, :], ident[0:2 * H, H:2 * H], smax[:, 0:1], None, ALU.mult).then_inc(diag_done, 1)

            def exponents(n):
                dve.wait_ge(m_ps, n + 1)
                v.tensor_copy(m_bc[:, :], fps[:, 0:H]).then_inc(m_done, 1)
                dve.wait_ge(m_done, n + 1)
                m = m_bc[:, :].rearrange("p (a h) -> p a h", a=1).broadcast_to([P, T, H])
                if not is_zero(n):
                    dve.wait_ge(exp_done, n * 2)
                v.tensor_tensor(expo[:, 0, :, :], sn[:, :, H:2 * H], m, ALU.subtract).then_inc(expo_step, 1)
                v.tensor_tensor(expo[:, 2, :, :], sn[:, :, 0:H], m, ALU.add).then_inc(expo_step, 1)
                dve.wait_ge(expo_step, n * 4 + 2)
                v.tensor_scalar(expo[:, 1, :, :], expo[:, 0, :, :], SLOPE, None, ALU.mult).then_inc(expo_step, 1)
                v.tensor_scalar(expo[:, 2, :, :], expo[:, 2, :, :], RHO_CAP, 1.0 - SLOPE, ALU.min, ALU.mult).then_inc(expo_step, 1)

            def values(n, p):
                dve.wait_ge(wh_ps, n + 1)
                dve.wait_ge(exp_done, n * 2 + 2)
                wh = fps[:, :].rearrange("p (q c) -> p q c", c=DH)
                q = xp[p][:, :, :, 0, :].rearrange("p t h c -> p (t h) c")
                for c in range(2):
                    f = bd[:, c, :, :].rearrange("p t (h a) -> p (t h) a", a=1)
                    v.tensor_tensor(q[:, :, c * V:c * V + DH], wh, f.broadcast_to([P, T * H, DH]), ALU.mult).then_inc(values_done, 1)
                    v.tensor_copy(q[:, :, c * V + DH:(c + 1) * V], f).then_inc(values_done, 1)

            def split(n, p):
                w = [xp[p][:, :, :, a, :].rearrange("p t h c -> p (t h) c") for a in range(PARTS)]
                up = [xp16[p][:, :, :, a, :].rearrange("p t h c -> p (t h) c") for a in range(PARTS)]
                dve.wait_ge(values_done, (n + 1) * 4)
                v.tensor_tensor(w[1], w[0], up[0], ALU.subtract).then_inc(rest1, 1)
                dve.wait_ge(rest1, n + 1)
                v.tensor_tensor(w[2], w[1], up[1], ALU.subtract).then_inc(xp_done, 1)

            def combine(n, p):
                dve.wait_ge(sumg_done, (n + 1) * H)
                dve.wait_ge(summ_done, (n + 1) * (T // 2))
                sg = sumg[p][:, :, :, :].rearrange("p t h c -> p (t h) c")
                sm = summ[p][:, :, :].rearrange("p t (h c) -> p (t h) c", c=V)
                r = rho[p][:, :, :].rearrange("p t (h a) -> p (t h) a", a=1).broadcast_to([P, T * H, V])
                v.tensor_scalar(lone[:, :], summ[p][:, :, DH], 0.0, None, ALU.is_equal).then_inc(p_lone, 1)
                v.tensor_tensor(num[:, :, :], sg[:, :, 0:V], r, ALU.mult).then_inc(p_rho, 1)
                dve.wait_ge(p_lone, n + 1)
                v.tensor_tensor(sm, sm, sg[:, :, V:C], ALU.subtract).then_inc(p_sub, 1)
                dve.wait_ge(p_rho, n + 1)
                dve.wait_ge(p_sub, n + 1)
                v.tensor_tensor(num[:, :, :], num[:, :, :], sm, ALU.add).then_inc(p_add, 1)

            def mend(n, p):
                dve.wait_ge(p_add, n + 1)
                dve.wait_ge(wsum_done, n + 1)
                nt = num[:, :, :].rearrange("p (t h) c -> p t (h c)", t=T)
                for t in range(T):
                    v.scalar_tensor_tensor(nt[:, t, :], wsum[p][:, :, :].rearrange("p h c -> p (h c)"), lone[:, t:t + 1],
                                           nt[:, t, :], ALU.mult, ALU.add).then_inc(p_fix, 1)

            def normalise(n):
                dve.wait_ge(p_fix, (n + 1) * T)
                v.reciprocal(rden[:, :], num[:, :, DH]).then_inc(p_rden, 1)
                dve.wait_ge(p_rden, n + 1)
                v.tensor_tensor(agg[:, :, :].rearrange("p t (h c) -> p (t h) c", c=DH), num[:, :, 0:DH],
                                rden[:, :].rearrange("p (q a) -> p q a", a=1).broadcast_to([P, T * H, DH]),
                                ALU.mult).then_inc(p_agg, 1)

            def out_stats(n):
                dve.wait_ge(p_agg, n + 1)
                for t in range(T):
                    v.bn_stats(stats2[:, t, :], agg[:, t, :]).then_inc(p_stats, 1)
                dve.wait_ge(p_stats, (n + 1) * T)
                settle(dve)
                for t in range(T):
                    v.bn_aggr(mv2[:, t, :], stats2[:, t, :]).then_inc(p_mv, 1)
                dve.wait_ge(p_mv, (n + 1) * T)
                v.tensor_scalar(var2[:, :], mv2[:, :, 1], EPS, None, ALU.add).then_inc(p_var, 1)

            def out_norm(n):
                for t in range(T):
                    v.scalar_tensor_tensor(agg[:, t, :], agg[:, t, :], mv2[:, t, 0:1], gam[:, :], ALU.subtract,
                                           ALU.mult).then_inc(p_gam, 1)

            def out_beta(n):
                dve.wait_ge(p_rs, n + 1)
                dve.wait_ge(p_gam, (n + 1) * T)
                for t in range(T):
                    v.scalar_tensor_tensor(agg[:, t, :], agg[:, t, :], rs2[:, t:t + 1], bet[:, :], ALU.mult,
                                           ALU.add).then_inc(p_z, 1)

            def out_elu(n):
                dve.wait_ge(p_z, (n + 1) * T)
                dve.wait_ge(x_res_ld, (n + 1) * 16)
                v.scalar_tensor_tensor(x_res[:, :, :], agg[:, :, :], -1.0, x_res[:, :, :], ALU.max, ALU.add).then_inc(p_y, 1)
                dve.wait_ge(p_y, n + 1)
                dve.wait_ge(p_exp, n + 1)
                v.scalar_tensor_tensor(x_res[:, :, :], e_out[:, :, :], 1.0, x_res[:, :, :], ALU.min, ALU.add).then_inc(p_out, 1)

            ln_in(0)
            dve.wait_ge(const_ld, 6 * 16)
            for c in range(2):
                v.tensor_tensor(wa_prod[:, c, :].rearrange("p (h d) -> p h d", h=H),
                                w_sb[:, :].rearrange("p (h d) -> p h d", h=H),
                                a12[:, c:c + 1, :].broadcast_to([P, H, DH]), ALU.mult).then_inc(ws_prod, 1)
            dve.wait_ge(ws_prod, 2)
            v.tensor_reduce(w_s[:, :], wa_prod[:, :, :].rearrange("p c (h d) -> p (c h) d", h=H), axis=AX.X,
                            op=ALU.add).then_inc(ws_done, 1)
            v.tensor_scalar(bet[:, :], bet[:, :], -1.0, None, ALU.add).then_inc(ws_done, 1)
            ln_out(0)
            mask_out(0, 0, 0)
            keep_scores(0, 0)
            mask_out(0, 0, 1)
            row_max(0)
            exponents(0)
            values(0, 0)
            split(0, 0)
            gen(0, 0, 0)

            def batch(b, p, front, post):
                for h in range(H):
                    if h < H - 1:
                        gen(b, p, h + 1)
                    mask_g(b, p, h)
                    if front:
                        if h == 0:
                            ln_in(b + 1)
                        if h == 2:
                            keep_scores(b + 1, 1 - p)
                        if h == 5:
                            exponents(b + 1)
                    if h:
                        sum_parts(b, p, h - 1)
                    if 0 < h <= T // 2:
                        sum_mterm(b, p, h - 1)
                    if front:
                        if h == 4:
                            row_max(b + 1)
                        if h == 5:
                            mask_out(b + 1, 1 - p, 0)
                        if h == 6:
                            values(b + 1, 1 - p)
                        if h == 7:
                            mask_out(b + 1, 1 - p, 1)
                            split(b + 1, 1 - p)
                            gen(b + 1, 1 - p, 0)
                    if post:
                        if h == 0:
                            combine(b - 1, 1 - p)
                    if front and h == 0:
                        ln_out(b + 1)
                    if post:
                        if h == 0:
                            mend(b - 1, 1 - p)
                        if h == 1:
                            normalise(b - 1)
                        if h == 2:
                            out_stats(b - 1)
                            out_norm(b - 1)
                        if h == 3:
                            out_beta(b - 1)
                        if h == 6:
                            out_elu(b - 1)
                sum_parts(b, p, H - 1)

            each_batch(dve, batch)
            combine(Bn - 1, 1)
            mend(Bn - 1, 1)
            normalise(Bn - 1)
            out_stats(Bn - 1)
            out_norm(Bn - 1)
            out_beta(Bn - 1)
            out_elu(Bn - 1)


_INS = ['x', 'adj', 'L0_gnn_W', 'L0_gnn_a1', 'L0_gnn_a2', 'L0_gnn_edge_emb', 'L0_gnn_ln_gamma', 'L0_gnn_ln_beta']


def kernel(**inputs):
    import concourse.bacc as _bacc
    from concourse.bass_utils import run_bass_kernel_spmd as _run

    nc = _bacc.Bacc("TRN2", target_bir_lowering=False, num_devices=1)
    arrays, args = {}, []
    for name in _INS:
        a = np.ascontiguousarray(inputs[name])
        arrays[f"in_{name}_dram"] = a
        args.append(nc.dram_tensor(f"in_{name}_dram", a.shape, mybir.dt.from_np(a.dtype), kind="ExternalInput").ap())
    o = nc.dram_tensor("out_0_dram", inputs['x'].shape, F32, kind="ExternalOutput").ap()
    gat_block(nc, *args, o)
    r = _run(nc, [arrays], core_ids=[0])
    return r.results[0]["out_0_dram"]
```

```python
import numpy as np
import concourse.bass as bass
from concourse import mybir
from contextlib import ExitStack

F32 = mybir.dt.float32
BF16 = mybir.dt.bfloat16
FP8 = mybir.dt.float8e4
U32 = mybir.dt.uint32
U8 = mybir.dt.uint8
ALU = mybir.AluOpType
ACT = mybir.ActivationFunctionType
AX = mybir.AxisListType


def gat_block(nc, x, adj, W, a1, a2, edge_emb, gamma, beta, out):
    Bn, N, F = x.shape
    H = edge_emb.shape[1]
    DH = F // H
    P = 128
    T = N // P
    R = 4
    K = T // R
    V = DH + 1
    C = 2 * V
    PARTS = 3
    CP = PARTS * C
    PITCH = 128
    BANK = 512
    NG = 4
    SLOPE = 0.2
    EPS = 1e-5
    BIG = float(2 ** 60)
    RHO_CAP = 100.0
    FIRST = [0, 1, 3, 3, 2, 2, 1, 1]
    MID = [1, 1, 1, 1, 0, 1, 1, 1]
    LAST = [1, 1, 1, 1, 1, 0, 2, 2]
    SUM_CUTS = [0, 5, 7]
    MEAN_CUTS = [0, 7]
    assert LAST[:2] == MID[:2]

    def dve_tiles(b):
        return (FIRST if b == 0 else LAST if b == Bn - 1 else MID) if isinstance(b, int) else MID

    def act_tiles(b):
        return [T - u for u in dve_tiles(b)]

    def count(tiles, b, h):
        if isinstance(b, int) and b == 0:
            return sum(tiles(0)[:h + 1])
        return sum(tiles(0)) + (b - 1) * sum(tiles(1)) + sum(tiles(b)[:h + 1])

    s1_rows = nc.dram_tensor("s1_rows", (2, H, N), F32, kind="Internal").ap()

    ctx = ExitStack()
    with ctx:
        def sb(name, shape, dt):
            return ctx.enter_context(nc.sbuf_tensor(name, shape, dt))

        def pb(name, shape, dt):
            return ctx.enter_context(nc.psum_tensor(name, shape, dt))

        def sem(name):
            return ctx.enter_context(nc.semaphore(name))

        ident = sb("ident", [P, P], F32)
        ones = sb("ones", [H, P], F32)
        minus_half = sb("minus_half", [P, T], F32)
        w_sb = sb("w_sb", [P, F], F32)
        a12 = sb("a12", [P, 2, DH], F32)
        wa_prod = sb("wa_prod", [P, 2, F], F32)
        w_s = sb("w_s", [P, 2 * H], F32)
        w_rep = sb("w_rep", [P, 2, P], F32)
        edge = sb("edge", [P, H], F32)
        gam = sb("gam", [P, F], F32)
        bet = sb("bet", [P, F], F32)
        x_ln = sb("x_ln", [P, T, F], F32)
        x_res = sb("x_res", [P, T, F], F32)
        stats = sb("stats", [P, T, 6], F32)
        mv = sb("mv", [P, T, 2], F32)
        var = sb("var", [P, T], F32)
        rs = sb("rs", [P, T], F32)
        xn = sb("xn", [P, T, F], F32)
        hT = sb("hT", [P, N], F32)
        hsum = sb("hsum", [P, 1], F32)
        hsum_rep = sb("hsum_rep", [P, P], F32)
        sn = sb("sn", [P, T, 2 * H], F32)
        thr = [sb(f"thr{p}", [P, T, H], F32) for p in range(2)]
        bigs2 = [sb(f"bigs2{p}", [P, T, H], F32) for p in range(2)]
        wsum = [sb(f"wsum{p}", [P, H, V], F32) for p in range(2)]
        sT = sb("sT", [H, N], F32)
        tmax = sb("tmax", [P, H], F32)
        smax = sb("smax", [H, 1], F32)
        smax_diag = sb("smax_diag", [H, H], F32)
        m_bc = sb("m_bc", [P, H], F32)
        expo = sb("expo", [P, 3, T, H], F32)
        bd = sb("bd", [P, 2, T, H], F32)
        rho = [sb(f"rho{p}", [P, T, H], F32) for p in range(2)]
        s1bc = sb("s1bc", [P, H, N], F32)
        xp = [sb(f"xp{p}", [P, T, H, PARTS, C], F32) for p in range(2)]
        adj8 = sb("adj8", [P, T, N], U8)
        mask = [sb(f"mask{p}", [P, K, N], U32) for p in range(2)]
        g = sb("g", [P, NG, K, N], U32)
        sumg = [sb(f"sumg{p}", [P, T, H, C], F32) for p in range(2)]
        summ = [sb(f"summ{p}", [P, T, H * V], F32) for p in range(2)]
        lone = sb("lone", [P, T], F32)
        num = sb("num", [P, T * H, V], F32)
        rden = sb("rden", [P, T * H], F32)
        agg = sb("agg", [P, T, F], F32)
        stats2 = sb("stats2", [P, T, 6], F32)
        mv2 = sb("mv2", [P, T, 2], F32)
        var2 = sb("var2", [P, T], F32)
        rs2 = sb("rs2", [P, T], F32)
        e_out = sb("e_out", [P, T, F], F32)

        acc = [pb(f"acc{q}", [P, T, PITCH], F32) for q in range(2)]
        mps = pb("mps", [P, 2, BANK], F32)
        fps = pb("fps", [P, 2 * BANK], F32)

        acc_flat = [a[:, :, :].rearrange("p t c -> p (t c)") for a in acc]
        mps_flat = mps[:, :, :].rearrange("p a c -> p (a c)")
        g8 = g[:, :, :, :].bitcast(FP8).rearrange("p n k (i r) -> p n k i r", r=R)
        mask8 = [m[:, :, :].bitcast(FP8).rearrange("p k (i r) -> p k i r", r=R) for m in mask]
        xp16 = [q[:, :, :, :, :].bitcast(BF16).rearrange("p t h a (c w) -> p t h a c w", w=2)[:, :, :, :, :, 1]
                for q in xp]
        adj_w = adj8[:, :, :].bitcast(F32)

        const_ld = sem("const_ld")
        x_ln_ld = sem("x_ln_ld")
        x_res_ld = sem("x_res_ld")
        adj_ld = sem("adj_ld")
        s1_st = sem("s1_st")
        s1bc_ld = [sem(f"s1bc_ld{q}") for q in range(H // 2)]
        out_st = sem("out_st")
        ident_zero = sem("ident_zero")
        consts = sem("consts")
        waits_met = sem("waits_met")
        ws_prod = sem("ws_prod")
        ws_done = sem("ws_done")
        bet_done = sem("bet_done")
        w_rep_done = sem("w_rep_done")
        ln_stats = sem("ln_stats")
        ln_mv = sem("ln_mv")
        ln_var = sem("ln_var")
        ln_rs = sem("ln_rs")
        ln_done = sem("ln_done")
        hT_ps = sem("hT_ps")
        hT_done = sem("hT_done")
        hrep_done = sem("hrep_done")
        s_ps = sem("s_ps")
        sT_ps = sem("sT_ps")
        s1_kept = sem("s1_kept")
        s2_kept = sem("s2_kept")
        thr_done = sem("thr_done")
        wsum_done = sem("wsum_done")
        tmax_done = sem("tmax_done")
        tmax_ps = sem("tmax_ps")
        sT_done = sem("sT_done")
        smax_done = sem("smax_done")
        diag_done = sem("diag_done")
        m_ps = sem("m_ps")
        m_done = sem("m_done")
        expo_step = sem("expo_step")
        exp_done = sem("exp_done")
        wh_ps = sem("wh_ps")
        values_done = sem("values_done")
        rest1 = sem("rest1")
        xp_done = sem("xp_done")
        mask_ps = sem("mask_ps")
        mask_done = sem("mask_done")
        gen_act = sem("gen_act")
        gen_dve = sem("gen_dve")
        bcast_ps = sem("bcast_ps")
        g_done = sem("g_done")
        acc_done = sem("acc_done")
        sumg_done = sem("sumg_done")
        mterm_ps = sem("mterm_ps")
        summ_done = sem("summ_done")
        lone_done = sem("lone_done")
        p_sub = sem("p_sub")
        p_rho = sem("p_rho")
        p_add = sem("p_add")
        p_rden = sem("p_rden")
        p_agg = sem("p_agg")
        p_stats = sem("p_stats")
        p_mv = sem("p_mv")
        p_var = sem("p_var")
        p_rs = sem("p_rs")
        p_gam = sem("p_gam")
        p_z = sem("p_z")
        p_exp = sem("p_exp")
        p_y = sem("p_y")
        p_out = sem("p_out")

        def nodes(ap2d):
            return ap2d.rearrange("(k p r) f -> p k r f", k=K, p=P)

        def tiles(t):
            return t.rearrange("p (k r) f -> p k r f", k=K)

        def graph(ap, b):
            return ap[b, :, :] if isinstance(b, int) else ap[bass.ds(b, 1), :, :].rearrange("a n f -> (a n) f")

        block = ctx.enter_context(nc.Block())

        def settle(eng):
            eng.sem_inc(waits_met, 1)

        def is_zero(n):
            return isinstance(n, int) and n == 0

        def each_batch(eng, batch):
            batch(0, 0, True, False)
            with eng.Fori(0, Bn // 2 - 1) as i:
                batch(i * 2 + 1, 1, True, True)
                batch(i * 2 + 2, 0, True, True)
            batch(Bn - 1, 1, False, True)

        @block.sync
        def _(sp):
            sp.dma_start(x_ln[:, :, :].rearrange("p (k r) f -> p k r f", k=K), nodes(x[0, :, :])).then_inc(x_ln_ld, 16)
            sp.dma_start(w_sb[:, :], W).then_inc(const_ld, 16)
            for c, v in enumerate((a1, a2)):
                sp.dma_start(a12[:, c, :], v.rearrange("(a d) -> a d", a=1).broadcast_to([P, DH])).then_inc(const_ld, 16)
            sp.dma_start(edge[:, :], edge_emb[1:2, :].broadcast_to([P, H])).then_inc(const_ld, 16)
            for t_, v in ((gam, gamma), (bet, beta)):
                sp.dma_start(t_[:, :], v.rearrange("(a d) -> a d", a=1).broadcast_to([P, F])).then_inc(const_ld, 16)

            def scores_out(n, p):
                sp.wait_ge(sT_done, n + 1)
                sp.dma_start(s1_rows[p, :, :], sT[:, :]).then_inc(s1_st, 16)
                sp.wait_ge(s1_st, (n + 1) * 16)
                for q in range(H // 2):
                    if not is_zero(n):
                        sp.wait_ge(gen_act, count(act_tiles, n - 1, 2 * q + 1))
                        settle(sp)
                        sp.wait_ge(gen_dve, count(dve_tiles, n - 1, 2 * q + 1))
                        settle(sp)
                    sp.dma_start(s1bc[:, 2 * q:2 * q + 2, :],
                                 s1_rows[p:p + 1, 2 * q:2 * q + 2, :].broadcast_to([P, 2, N])).then_inc(s1bc_ld[q], 16)

            def load_x_ln(n):
                sp.wait_ge(ln_done, n)
                sp.dma_start(tiles(x_ln[:, :, :]), nodes(graph(x, n))).then_inc(x_ln_ld, 16)

            def store_out(n):
                sp.wait_ge(p_out, n + 1)
                sp.dma_start(nodes(graph(out, n)), tiles(x_res[:, :, :])).then_inc(out_st, 16)

            def load_x_res(n):
                if not is_zero(n):
                    sp.wait_ge(out_st, n * 16)
                sp.dma_start(tiles(x_res[:, :, :]), nodes(graph(x, n))).then_inc(x_res_ld, 16)

            load_x_ln(1)
            scores_out(0, 0)

            def batch(b, p, front, post):
                if front:
                    if not is_zero(b):
                        load_x_ln(b + 1)
                    scores_out(b + 1, 1 - p)
                if post:
                    store_out(b - 1)
                load_x_res(b)

            each_batch(sp, batch)
            for k in range(K):
                sp.wait_ge(p_out, Bn + k)
                sp.dma_start(nodes(out[Bn - 1, :, :])[:, k, :, :], tiles(x_res[:, :, :])[:, k, :, :]).then_inc(out_st, 16)
            sp.wait_ge(out_st, (Bn - 1 + K) * 16)

        @block.gpsimd
        def _(pool):
            pool.memset(ident[:, :], 0.0).then_inc(ident_zero, 1)
            pool.memset(ones[:, :], 1.0).then_inc(consts, 1)
            pool.memset(minus_half[:, :], -0.5).then_inc(consts, 1)
            pool.wait_ge(ident_zero, 1)
            pool.affine_select(out=ident[:, :], in_=ident[:, :], compare_op=ALU.not_equal, fill=1.0, base=0,
                               pattern=[[-1, P]], channel_multiplier=1).then_inc(consts, 1)
            for w in wsum:
                pool.memset(w[:, :, DH:V], float(N)).then_inc(consts, 1)

            def load_adj(n):
                pool.dma_start(tiles(adj8[:, :, :]), nodes(graph(adj, n))).then_inc(adj_ld, 16)

            def inverse_roots(n, var_done, var_, rs_, done):
                pool.wait_ge(var_done, n + 1)
                pool.tensor_tensor(rs_[:, :], var_[:, :], minus_half[:, :], ALU.pow).then_inc(done, 1)

            load_adj(0)
            pool.wait_ge(consts, 5)
            inverse_roots(0, ln_var, var, rs, ln_rs)
            inverse_roots(1, ln_var, var, rs, ln_rs)

            def batch(b, p, front, post):
                if front:
                    pool.wait_ge(mask_ps, (b + 1) * K)
                    if is_zero(b):
                        pool.wait_ge(s1bc_ld[0], 16)
                    load_adj(b + 1)
                if front and not is_zero(b):
                    inverse_roots(b + 1, ln_var, var, rs, ln_rs)
                if post:
                    inverse_roots(b - 1, p_var, var2, rs2, p_rs)

            each_batch(pool, batch)
            inverse_roots(Bn - 1, p_var, var2, rs2, p_rs)

        @block.tensor
        def _(pe):
            pe.wait_ge(consts, 5)

            def mask_transpose(n, k):
                if k:
                    pe.wait_ge(mask_done, n * K + k)
                else:
                    pe.wait_ge(adj_ld, (n + 1) * 16)
                    if not is_zero(n):
                        pe.wait_ge(summ_done, n * T)
                for t in range(T):
                    last = nc.tensor.transpose(mps_flat[:, t * P:(t + 1) * P], adj_w[:, t, k * P:(k + 1) * P], ident[:, :])
                last.then_inc(mask_ps, 1)

            def h_transpose(n):
                pe.wait_ge(ln_done, n + 1)
                if not is_zero(n):
                    pe.wait_ge(values_done, n * 4)
                for t in range(T):
                    last = nc.tensor.transpose(fps[:, t * P:(t + 1) * P], xn[:, t, :], ident[:, :])
                last.then_inc(hT_ps, 1)

            def scores_by_row(n, ps):
                if not is_zero(n):
                    pe.wait_ge(hT_done, n + 1)
                for c in range(N // BANK):
                    last = nc.tensor.matmul(ps[0:H, c * BANK:(c + 1) * BANK], w_s[:, 0:H], hT[:, c * BANK:(c + 1) * BANK],
                                            start=True, stop=True)
                last.then_inc(sT_ps, 1)

            def scores_on_all(h):
                pe.wait_ge(w_rep_done, h + 1)
                for c in range(N // BANK):
                    last = nc.tensor.matmul(acc_flat[h][:, c * BANK:(c + 1) * BANK], w_rep[:, h, :],
                                            hT[:, c * BANK:(c + 1) * BANK], start=True, stop=True)
                last.then_inc(bcast_ps, 1)

            def scores(n):
                if not is_zero(n):
                    pe.wait_ge(sT_done, n + 1)
                for t in range(T):
                    nc.tensor.matmul(fps[:, t * 2 * H:(t + 1) * 2 * H], hT[:, t * P:(t + 1) * P], w_s[:, :],
                                     start=True, stop=True)
                pe.wait_ge(hrep_done, n + 1)
                nc.tensor.matmul(fps[:, P:2 * P], hsum_rep[:, :], w_sb[:, :], start=True, stop=True).then_inc(s_ps, 1)

            def maxima_by_row(n, ps):
                pe.wait_ge(tmax_done, n + 1)
                pe.wait_ge(wsum_done, n + 1)
                nc.tensor.transpose(ps[0:H, 0:P], tmax[:, :], ident[:, :]).then_inc(tmax_ps, 1)

            def largest(n, ps):
                pe.wait_ge(diag_done, n + 1)
                nc.tensor.matmul(ps[:, 0:H], ones[:, :], smax_diag[:, :], start=True, stop=True).then_inc(m_ps, 1)

            def node_values(n, t0, t1):
                for t in range(t0, t1):
                    last = nc.tensor.matmul(fps[:, t * F:(t + 1) * F], hT[:, t * P:(t + 1) * P], w_sb[:, :],
                                            start=True, stop=True)
                last.then_inc(wh_ps, 1)

            def head(b, p, h):
                n = b * H + h
                pe.wait_ge(g_done, n + 1)
                if h >= 2 or not is_zero(b):
                    pe.wait_ge(sumg_done, n - 1)
                settle(pe)
                for t in range(T):
                    for j in range(T):
                        last = nc.tensor.matmul(acc[h % 2][:, t, 0:CP].rearrange("p (a c) -> p a c", a=PARTS),
                                                g8[:, h % NG, j // R, t * P:(t + 1) * P, j % R],
                                                xp16[p][:, j, h, :, :],
                                                start=(j == 0), stop=(j == T - 1))
                last.then_inc(acc_done, 1)

            def mterm(b, p, q):
                if q:
                    pe.wait_ge(summ_done, b * T + 2 * q)
                else:
                    pe.wait_ge(mask_done, (b + 1) * K)
                settle(pe)
                for c in range(2):
                    t = 2 * q + c
                    for j in range(T):
                        for a in range(PARTS):
                            last = nc.tensor.matmul(mps[:, c, 0:H * V].rearrange("p (h c) -> p h c", h=H),
                                                    mask8[p][:, j // R, t * P:(t + 1) * P, j % R],
                                                    xp16[p][:, j, :, a, V:C],
                                                    start=(j == 0 and a == 0), stop=(j == T - 1 and a == PARTS - 1))
                last.then_inc(mterm_ps, 1)

            mask_transpose(0, 0)
            h_transpose(0)
            pe.wait_ge(hT_done, 1)
            pe.wait_ge(ws_done, 1)
            scores_by_row(0, acc_flat[1])
            scores(0)
            scores_on_all(0)
            maxima_by_row(0, fps[:, BANK:])
            largest(0, fps[:, BANK:])
            node_values(0, 0, T // 2)
            pe.wait_ge(m_done, 1)
            node_values(0, T // 2, T)
            mask_transpose(0, 1)
            pe.wait_ge(sT_done, 1)
            scores_on_all(1)

            def batch(b, p, front, post):
                pe.wait_ge(xp_done, b + 1)
                for h in range(H):
                    head(b, p, h)
                    if front:
                        if h == 0:
                            h_transpose(b + 1)
                        elif h == 1:
                            scores_by_row(b + 1, fps)
                        elif h == 2:
                            scores(b + 1)
                        elif h == 3:
                            maxima_by_row(b + 1, fps)
                        elif h == 4:
                            largest(b + 1, fps)
                            mask_transpose(b + 1, 0)
                        elif h == 5:
                            pe.wait_ge(m_done, b + 2)
                            node_values(b + 1, 0, T)
                        elif h == 6:
                            mask_transpose(b + 1, 1)
                    if h < T // 2:
                        mterm(b, p, h)

            each_batch(pe, batch)

        @block.scalar
        def _(act):
            def gen(b, p, h, between=None, at=T // 2):
                n = b * H + h
                first = isinstance(b, int) and b == 0
                in_ps = first and h < 2
                if in_ps:
                    act.wait_ge(bcast_ps, h + 1)
                else:
                    act.wait_ge(s1bc_ld[h // 2], (b + 1) * 16)
                if h == 0:
                    act.wait_ge(thr_done, (b + 1) * 2)
                if not (first and h < NG):
                    act.wait_ge(acc_done, n - NG + 1)
                settle(act)
                s1 = acc_flat[h] if in_ps else s1bc[:, h, :]
                for j in range(dve_tiles(b)[h], T):
                    if between and j == at:
                        between()
                        settle(act)
                    nc.scalar.activation(g8[:, h % NG, j // R, :, j % R], s1, ACT.Relu,
                                         bias=bigs2[p][:, j, h:h + 1], scale=BIG, saturate=False).then_inc(gen_act, 1)

            def h_out(n):
                act.wait_ge(hT_ps, n + 1)
                nc.scalar.activation(hT[:, :], fps[:, :], ACT.Relu, accum_out=hsum[:, :]).then_inc(hT_done, 1)

            def h_rep(n):
                act.wait_ge(hT_done, n + 1)
                nc.scalar.activation(hsum_rep[:, :], hsum[:, :].broadcast_to([P, P]), ACT.Copy).then_inc(hrep_done, 1)

            def rows_out(n, ps):
                act.wait_ge(sT_ps, n + 1)
                if not is_zero(n):
                    act.wait_ge(s1_st, n * 16)
                nc.scalar.activation(sT[:, :], ps[0:H, :], ACT.Copy).then_inc(sT_done, 1)

            def exps(n, p):
                act.wait_ge(expo_step, (n + 1) * 4)
                nc.scalar.activation(bd[:, :, :, :], expo[:, 0:2, :, :], ACT.Exp).then_inc(exp_done, 1)
                nc.scalar.activation(rho[p][:, :, :], expo[:, 2, :, :], ACT.Exp).then_inc(exp_done, 1)

            def out_exp(n):
                act.wait_ge(p_z, (n + 1) * T)
                nc.scalar.activation(e_out[:, :, :], agg[:, :, :], ACT.Exp, bias=1.0).then_inc(p_exp, 1)

            act.wait_ge(ws_done, 1)
            for h in range(2):
                nc.scalar.activation(w_rep[:, h, :], w_s[:, h:h + 1].broadcast_to([P, P]), ACT.Copy).then_inc(w_rep_done, 1)
            h_out(0)
            h_rep(0)
            rows_out(0, acc_flat[1])
            gen(0, 0, 0, lambda: exps(0, 0), 2)
            gen(0, 0, 1)

            def batch(b, p, front, post):
                for h in range(H):
                    step = None
                    if front and h == 1:
                        step = lambda: (h_out(b + 1), h_rep(b + 1))
                    if front and h == 2:
                        step = lambda: rows_out(b + 1, fps)
                    if post and h == (4 if front else 5):
                        step = lambda: out_exp(b - 1)
                    at = T // 2
                    if front and h == 5:
                        step = lambda: exps(b + 1, 1 - p)
                        at = T - 1 if is_zero(b) else 2
                    if h == 1:
                        at = T - 1
                    if h < H - 2:
                        gen(b, p, h + 2, step, at)
                    elif front:
                        gen(b + 1, 1 - p, h + 2 - H, step)

            each_batch(act, batch)
            for k in range(K):
                act.wait_ge(p_z, (Bn - 1) * T + (k + 1) * R)
                nc.scalar.activation(e_out[:, k * R:(k + 1) * R, :], agg[:, k * R:(k + 1) * R, :], ACT.Exp,
                                     bias=1.0).then_inc(p_exp, 1)

        @block.vector
        def _(dve):
            v = nc.vector

            def gen(b, p, h):
                n = b * H + h
                first = isinstance(b, int) and b == 0
                if not dve_tiles(b)[h]:
                    return
                dve.wait_ge(s1bc_ld[h // 2], (b + 1) * 16)
                if not (first and h < NG):
                    dve.wait_ge(acc_done, n - NG + 1)
                settle(dve)
                for j in range(dve_tiles(b)[h]):
                    v.tensor_scalar(g8[:, h % NG, j // R, :, j % R], s1bc[:, h, :], thr[p][:, j, h:h + 1], None,
                                    ALU.is_gt, saturate=False).then_inc(gen_dve, 1)

            def mask_g(b, p, h):
                dve.wait_ge(gen_act, count(act_tiles, b, h))
                if not is_zero(count(dve_tiles, b, h)):
                    dve.wait_ge(gen_dve, count(dve_tiles, b, h))
                if h == 0:
                    dve.wait_ge(mask_done, (b + 1) * K)
                v.tensor_tensor(g[:, h % NG, :, :], g[:, h % NG, :, :], mask[p][:, :, :], ALU.bitwise_and).then_inc(g_done, 1)

            def sum_parts(b, p, h):
                dve.wait_ge(acc_done, b * H + h + 1)
                v.tensor_reduce(sumg[p][:, :, h, :], acc[h % 2][:, :, 0:CP].rearrange("p t (a c) -> p t c a", a=PARTS),
                                axis=AX.X, op=ALU.add).then_inc(sumg_done, 1)

            def find_lone(b, q):
                dve.wait_ge(mterm_ps, b * (T // 2) + q + 1)
                v.tensor_scalar(lone[:, 2 * q:2 * q + 2], mps[:, :, DH], 0.0, None, ALU.is_equal).then_inc(lone_done, 1)

            def keep_mterm(b, p, q):
                dve.wait_ge(lone_done, b * (T // 2) + q + 1)
                if q == 0:
                    dve.wait_ge(wsum_done, b + 1)
                for c in range(2):
                    t = 2 * q + c
                    v.scalar_tensor_tensor(summ[p][:, t, :], wsum[p][:, :, :].rearrange("p h c -> p (h c)"), lone[:, t:t + 1],
                                           mps[:, c, 0:H * V], ALU.mult, ALU.add).then_inc(summ_done, 1)

            def mask_out(n, p, k):
                dve.wait_ge(mask_ps, n * K + k + 1)
                v.tensor_scalar(mask[p][:, k, :], mps_flat.bitcast(U32), 3, None,
                                ALU.logical_shift_left).then_inc(mask_done, 1)

            def ln_in(n):
                dve.wait_ge(x_ln_ld, (n + 1) * 16)
                for t in range(T):
                    v.bn_stats(stats[:, t, :], x_ln[:, t, :]).then_inc(ln_stats, 1)
                dve.wait_ge(ln_stats, (n + 1) * T)
                settle(dve)
                for t in range(T):
                    v.bn_aggr(mv[:, t, :], stats[:, t, :]).then_inc(ln_mv, 1)
                dve.wait_ge(ln_mv, (n + 1) * T)
                v.tensor_scalar(var[:, :], mv[:, :, 1], EPS, None, ALU.add).then_inc(ln_var, 1)

            def ln_out(n):
                dve.wait_ge(ln_rs, n + 1)
                if not is_zero(n):
                    dve.wait_ge(hT_ps, n)
                for t in range(T):
                    last = v.tensor_scalar(xn[:, t, :], x_ln[:, t, :], mv[:, t, 0:1], rs[:, t:t + 1],
                                           ALU.subtract, ALU.mult)
                last.then_inc(ln_done, 1)

            def keep_scores(n, p):
                dve.wait_ge(s_ps, n + 1)
                if not (isinstance(n, int) and n < 2):
                    dve.wait_ge(summ_done, (n - 1) * T)
                s = fps[:, 0:2 * H * T].rearrange("p (t c) -> p t c", t=T)
                v.tensor_tensor(sn[:, :, H:2 * H], s[:, :, H:2 * H],
                                edge[:, :].rearrange("p (a h) -> p a h", a=1).broadcast_to([P, T, H]), ALU.add).then_inc(s2_kept, 1)
                v.tensor_copy(sn[:, :, 0:H], s[:, :, 0:H]).then_inc(s1_kept, 1)
                dve.wait_ge(s2_kept, n + 1)
                v.reduce_max(tmax[:, :], sn[:, :, H:2 * H].rearrange("p t h -> p h t"), axis=AX.X).then_inc(tmax_done, 1)
                v.tensor_copy(wsum[p][:, :, 0:DH], fps[:, P:2 * P].rearrange("p (h c) -> p h c", h=H)).then_inc(wsum_done, 1)
                v.tensor_scalar(thr[p][:, :, :], sn[:, :, H:2 * H], -1.0, None, ALU.mult).then_inc(thr_done, 1)
                v.tensor_scalar(bigs2[p][:, :, :], sn[:, :, H:2 * H], BIG, None, ALU.mult).then_inc(thr_done, 1)

            def row_max(n, ps=fps):
                dve.wait_ge(tmax_ps, n + 1)
                v.reduce_max(smax[:, :], ps[0:H, 0:P], axis=AX.X).then_inc(smax_done, 1)

            def max_diagonal(n):
                dve.wait_ge(smax_done, n + 1)
                v.tensor_scalar(smax_diag[:, :], ident[0:H, 0:H], smax[:, 0:1], None, ALU.mult).then_inc(diag_done, 1)

            def keep_max(n, ps=fps):
                dve.wait_ge(m_ps, n + 1)
                v.tensor_copy(m_bc[:, :], ps[:, 0:H]).then_inc(m_done, 1)

            def shift_scores(n):
                dve.wait_ge(m_done, n + 1)
                m = m_bc[:, :].rearrange("p (a h) -> p a h", a=1).broadcast_to([P, T, H])
                if not is_zero(n):
                    dve.wait_ge(exp_done, n * 2)
                dve.wait_ge(s1_kept, n + 1)
                v.tensor_tensor(expo[:, 0, :, :], sn[:, :, H:2 * H], m, ALU.subtract).then_inc(expo_step, 1)
                v.tensor_tensor(expo[:, 2, :, :], sn[:, :, 0:H], m, ALU.add).then_inc(expo_step, 1)

            def exponents(n):
                dve.wait_ge(expo_step, n * 4 + 2)
                v.tensor_scalar(expo[:, 1, :, :], expo[:, 0, :, :], SLOPE, None, ALU.mult).then_inc(expo_step, 1)
                v.tensor_scalar(expo[:, 2, :, :], expo[:, 2, :, :], RHO_CAP, 1.0 - SLOPE, ALU.min, ALU.mult).then_inc(expo_step, 1)

            def values(n, p):
                dve.wait_ge(wh_ps, n + 2)
                dve.wait_ge(exp_done, n * 2 + 2)
                wh = fps[:, :].rearrange("p (q c) -> p q c", c=DH)
                q = xp[p][:, :, :, 0, :].rearrange("p t h c -> p (t h) c")
                for c in range(2):
                    f = bd[:, c, :, :].rearrange("p t (h a) -> p (t h) a", a=1)
                    v.tensor_tensor(q[:, :, c * V:c * V + DH], wh, f.broadcast_to([P, T * H, DH]), ALU.mult).then_inc(values_done, 1)
                    v.tensor_copy(q[:, :, c * V + DH:(c + 1) * V], f).then_inc(values_done, 1)

            def split(n, p):
                w = [xp[p][:, :, :, a, :].rearrange("p t h c -> p (t h) c") for a in range(PARTS)]
                up = [xp16[p][:, :, :, a, :].rearrange("p t h c -> p (t h) c") for a in range(PARTS)]
                dve.wait_ge(values_done, (n + 1) * 4)
                v.tensor_tensor(w[1], w[0], up[0], ALU.subtract).then_inc(rest1, 1)
                dve.wait_ge(rest1, n + 1)
                v.tensor_tensor(w[2], w[1], up[1], ALU.subtract).then_inc(xp_done, 1)

            def pieces_done(n, h0, cuts):
                return n + 1 + cuts.index(h0)

            def combine(n, p, h0=0, h1=H):
                done = pieces_done(n, h0, SUM_CUTS)
                dve.wait_ge(sumg_done, n * H + h1)
                dve.wait_ge(summ_done, (n + 1) * T)
                sg = sumg[p][:, :, h0:h1, :]
                sm = summ[p][:, :, :].rearrange("p t (h c) -> p t h c", c=V)[:, :, h0:h1, :]
                nm = num[:, :, :].rearrange("p (t h) c -> p t h c", t=T)[:, :, h0:h1, :]
                r = rho[p][:, :, h0:h1].rearrange("p t (h a) -> p t h a", a=1).broadcast_to([P, T, h1 - h0, V])
                v.tensor_tensor(nm, sg[:, :, :, 0:V], r, ALU.mult).then_inc(p_rho, 1)
                v.tensor_tensor(sm, sm, sg[:, :, :, V:C], ALU.subtract).then_inc(p_sub, 1)

            def add_up(n, p, h0=0, h1=H):
                done = pieces_done(n, h0, SUM_CUTS)
                nm = num[:, :, :].rearrange("p (t h) c -> p t h c", t=T)[:, :, h0:h1, :]
                sm = summ[p][:, :, :].rearrange("p t (h c) -> p t h c", c=V)[:, :, h0:h1, :]
                dve.wait_ge(p_rho, done)
                dve.wait_ge(p_sub, done)
                v.tensor_tensor(nm, nm, sm, ALU.add).then_inc(p_add, 1)

            def normalise(n, h0=0, h1=H):
                done = pieces_done(n, h0, MEAN_CUTS)
                dve.wait_ge(p_add, n + 1 if h1 - h0 == H else n + len([c for c in SUM_CUTS if c < h1]))
                nm = num[:, :, :].rearrange("p (t h) c -> p t h c", t=T)[:, :, h0:h1, :]
                rd = rden[:, :].rearrange("p (t h) -> p t h", t=T)[:, :, h0:h1]
                v.reciprocal(rd, nm[:, :, :, DH]).then_inc(p_rden, 1)
                dve.wait_ge(p_rden, done)
                v.tensor_tensor(agg[:, :, h0 * DH:h1 * DH].rearrange("p t (h c) -> p t h c", c=DH), nm[:, :, :, 0:DH],
                                rd.rearrange("p t (h a) -> p t h a", a=1).broadcast_to([P, T, h1 - h0, DH]),
                                ALU.mult).then_inc(p_agg, 1)

            def out_stats(n, pieces=1, between=None):
                dve.wait_ge(p_agg, n + pieces)
                for t in range(T):
                    v.bn_stats(stats2[:, t, :], agg[:, t, :]).then_inc(p_stats, 1)
                if between:
                    between()
                dve.wait_ge(p_stats, (n + 1) * T)
                settle(dve)
                for t in range(T):
                    v.bn_aggr(mv2[:, t, :], stats2[:, t, :]).then_inc(p_mv, 1)
                dve.wait_ge(p_mv, (n + 1) * T)
                v.tensor_scalar(var2[:, :], mv2[:, :, 1], EPS, None, ALU.add).then_inc(p_var, 1)

            def out_norm(n):
                for t in range(T):
                    v.scalar_tensor_tensor(agg[:, t, :], agg[:, t, :], mv2[:, t, 0:1], gam[:, :], ALU.subtract,
                                           ALU.mult).then_inc(p_gam, 1)

            def out_beta(n):
                dve.wait_ge(p_rs, n + 1)
                dve.wait_ge(bet_done, 1)
                dve.wait_ge(p_gam, (n + 1) * T)
                for t in range(T):
                    v.scalar_tensor_tensor(agg[:, t, :], agg[:, t, :], rs2[:, t:t + 1], bet[:, :], ALU.mult,
                                           ALU.add).then_inc(p_z, 1)

            def out_elu(n):
                dve.wait_ge(p_z, (n + 1) * T)
                dve.wait_ge(x_res_ld, (n + 1) * 16)
                last = isinstance(n, int) and n == Bn - 1
                for i, t in enumerate([slice(k * R, (k + 1) * R) for k in range(K)] if last else [slice(0, T)]):
                    v.scalar_tensor_tensor(x_res[:, t, :], agg[:, t, :], -1.0, x_res[:, t, :], ALU.max, ALU.add).then_inc(p_y, 1)
                    dve.wait_ge(p_y, n + 1 + i)
                    dve.wait_ge(p_exp, n + 1 + i)
                    v.scalar_tensor_tensor(x_res[:, t, :], e_out[:, t, :], 1.0, x_res[:, t, :], ALU.min, ALU.add).then_inc(p_out, 1)

            ln_in(0)
            dve.wait_ge(const_ld, 6 * 16)
            for c in range(2):
                v.tensor_tensor(wa_prod[:, c, :].rearrange("p (h d) -> p h d", h=H),
                                w_sb[:, :].rearrange("p (h d) -> p h d", h=H),
                                a12[:, c:c + 1, :].broadcast_to([P, H, DH]), ALU.mult).then_inc(ws_prod, 1)
            dve.wait_ge(ws_prod, 2)
            v.tensor_reduce(w_s[:, :], wa_prod[:, :, :].rearrange("p c (h d) -> p (c h) d", h=H), axis=AX.X,
                            op=ALU.add).then_inc(ws_done, 1)
            ln_out(0)
            v.tensor_scalar(bet[:, :], bet[:, :], -1.0, None, ALU.add).then_inc(bet_done, 1)
            mask_out(0, 0, 0)
            ln_in(1)
            keep_scores(0, 0)
            row_max(0, fps[:, BANK:])
            max_diagonal(0)
            keep_max(0, fps[:, BANK:])
            shift_scores(0)
            exponents(0)
            ln_out(1)
            mask_out(0, 0, 1)
            values(0, 0)
            split(0, 0)

            def pieces(h1):
                for cuts, sums in ((SUM_CUTS, True), (MEAN_CUTS, False)):
                    for h0, end in zip(cuts, cuts[1:] + [H]):
                        if end == h1 and sums:
                            combine(Bn - 1, 1, h0, h1)
                            add_up(Bn - 1, 1, h0, h1)
                        elif end == h1:
                            normalise(Bn - 1, h0, h1)

            def batch(b, p, front, post):
                for h in range(H):
                    q = h - 1
                    if h < H - 1:
                        gen(b, p, h + 1)
                    mask_g(b, p, h)
                    if h == 0:
                        if front and post:
                            ln_in(b + 1)
                        if post:
                            combine(b - 1, 1 - p)
                        if front and post:
                            ln_out(b + 1)
                        if post:
                            add_up(b - 1, 1 - p)
                    if front and h == 3:
                        keep_scores(b + 1, 1 - p)
                    if front and h == 5:
                        keep_max(b + 1)
                    if h:
                        sum_parts(b, p, h - 1)
                    if h == 1:
                        if post:
                            normalise(b - 1)
                        find_lone(b, q)
                        keep_mterm(b, p, q)
                    if h == 2:
                        if post:
                            out_stats(b - 1, 1, lambda: find_lone(b, q))
                            out_norm(b - 1)
                        else:
                            find_lone(b, q)
                        keep_mterm(b, p, q)
                    if h == 3:
                        find_lone(b, q)
                        if post:
                            out_beta(b - 1)
                        keep_mterm(b, p, q)
                    if h == 4:
                        if front:
                            row_max(b + 1)
                        find_lone(b, q)
                        if front:
                            max_diagonal(b + 1)
                        keep_mterm(b, p, q)
                    if front and h == 5:
                        shift_scores(b + 1)
                        mask_out(b + 1, 1 - p, 0)
                        exponents(b + 1)
                    if front and h == 6:
                        values(b + 1, 1 - p)
                    if post and h == 6:
                        out_elu(b - 1)
                    if front and h == 7:
                        mask_out(b + 1, 1 - p, 1)
                        split(b + 1, 1 - p)
                        gen(b + 1, 1 - p, 0)
                    if not front:
                        pieces(h)
                sum_parts(b, p, H - 1)

            each_batch(dve, batch)
            pieces(H)
            out_stats(Bn - 1, len(MEAN_CUTS))
            out_norm(Bn - 1)
            out_beta(Bn - 1)
            out_elu(Bn - 1)


_INS = ['x', 'adj', 'L0_gnn_W', 'L0_gnn_a1', 'L0_gnn_a2', 'L0_gnn_edge_emb', 'L0_gnn_ln_gamma', 'L0_gnn_ln_beta']


def kernel(**inputs):
    import concourse.bacc as _bacc
    from concourse.bass_utils import run_bass_kernel_spmd as _run

    nc = _bacc.Bacc("TRN2", target_bir_lowering=False, num_devices=1)
    arrays, args = {}, []
    for name in _INS:
        a = np.ascontiguousarray(inputs[name])
        arrays[f"in_{name}_dram"] = a
        args.append(nc.dram_tensor(f"in_{name}_dram", a.shape, mybir.dt.from_np(a.dtype), kind="ExternalInput").ap())
    o = nc.dram_tensor("out_0_dram", inputs['x'].shape, F32, kind="ExternalOutput").ap()
    gat_block(nc, *args, o)
    r = _run(nc, [arrays], core_ids=[0])
    return r.results[0]["out_0_dram"]
```
